# Optimizing a Trainium2 kernel written in Bass

```python
import numpy as np
import jax
import jax.numpy as jnp

def _softmax(x, axis=-1):
    return jax.nn.softmax(x, axis=axis)

def _gelu(x):
    return jax.nn.gelu(x, approximate=True)

def _silu(x):
    return jax.nn.silu(x)

def _sigmoid(x):
    return jax.nn.sigmoid(x)

def _layernorm(x, axis=-1, eps=1e-05):
    m = jnp.mean(x, axis=axis, keepdims=True)
    v = jnp.var(x, axis=axis, keepdims=True)
    return (x - m) / jnp.sqrt(v + eps)

def _scatter_add(tgt, idx, src, axis=0):
    return tgt.at[idx].add(src)

def _segment_sum(src, seg, n):
    return jax.ops.segment_sum(src, seg, n)
kernel_name = 'mk_flamingo_gated_d1_seqx_r4_7cdfb2'

def setup_inputs(seed: int=0):
    np.random.seed(seed)
    _w = jnp.asarray

    def _rec_inputs():
        import jax
        import jax.numpy as jnp
        _rk = jax.random.key(seed)
        x = -0.0002928 + 1 * jax.random.normal(jax.random.fold_in(_rk, 1), (8, 512, 256), jnp.float32)
        _lenS = 512 - jax.random.randint(jax.random.fold_in(_rk, 7), (8,), 0, max(1, 512 // 4) + 1, jnp.int32)
        _lenS2 = 512 - jax.random.randint(jax.random.fold_in(_rk, 8), (8,), 0, max(1, 512 // 4) + 1, jnp.int32)
        _ctx_512P = jax.random.normal(jax.random.fold_in(_rk, 11), (8, 16, 128), jnp.float32)
        _ctx_512c = jax.random.dirichlet(jax.random.fold_in(_rk, 511), 0.3 * jnp.ones((16,), jnp.float32), (8, 512))
        _ctx_512t = jnp.einsum('bsk,bkd->bsd', _ctx_512c, _ctx_512P)
        _ctx_512t = _ctx_512t * jax.lax.rsqrt(jnp.mean(jnp.square(_ctx_512t)) + 1e-12) * 0.953939
        ctx_512 = -1.52775e-05 + 0.999936 * (_ctx_512t + 0.3 * jax.random.normal(jax.random.fold_in(_rk, 611), (8, 512, 128), jnp.float32))
        _g = jax.random.normal(jax.random.fold_in(_rk, 9001), (2, 1), jnp.float32)
        _g = jnp.sign(_g) * jnp.maximum(jnp.abs(_g), 1.0) + (_g == 0) * 1.0
        g_xattn = _g[0]
        g_ffn = _g[1]
        return (x, ctx_512, g_xattn, g_ffn)
    x, ctx_512, g_xattn, g_ffn = _rec_inputs()

    def _L0_xattn_setup():
        import jax, jax.numpy as jnp
        import numpy as np
        NUM_HEADS = 16
        HEAD_DIM = 64
        Q_DIM = 256
        KV_DIM = 128
        INNER = NUM_HEADS * HEAD_DIM
        key = jax.random.key(seed)
        ks = jax.random.split(key, 7)
        B, N, M = (32, 128, 512)
        q = jax.random.normal(ks[0], (B, N, Q_DIM), dtype=jnp.float32)
        kv = jax.random.normal(ks[1], (B, M, KV_DIM), dtype=jnp.float32)
        Wq = jax.random.normal(ks[2], (Q_DIM, INNER), dtype=jnp.float32) / np.sqrt(Q_DIM)
        Wk = jax.random.normal(ks[3], (KV_DIM, INNER), dtype=jnp.float32) / np.sqrt(KV_DIM)
        Wv = jax.random.normal(ks[4], (KV_DIM, INNER), dtype=jnp.float32) / np.sqrt(KV_DIM)
        Wo = jax.random.normal(ks[5], (INNER, Q_DIM), dtype=jnp.float32) / np.sqrt(INNER)
        bo = jax.random.normal(ks[6], (Q_DIM,), dtype=jnp.float32) * 0.01
        return {'q': q, 'kv': kv, 'Wq': Wq, 'Wk': Wk, 'Wv': Wv, 'Wo': Wo, 'bo': bo}
    _L0_xattn_all = _L0_xattn_setup()
    _L0_xattn_in = {k: v for k, v in _L0_xattn_all.items() if k in ('Wq', 'Wk', 'Wv', 'Wo', 'bo')}
    del _L0_xattn_all

    def _L0_ffn_setup():
        import jax, jax.numpy as jnp
        import numpy as np
        TOP_K = 2
        N_EXPERTS = 8
        key = jax.random.key(seed)
        k1, k2, k3, k4 = jax.random.split(key, 4)
        B, C, L, O, E = (8, 1024, 256, 256, N_EXPERTS)
        scale = 1.0 / np.sqrt(L)
        return {'x': jax.random.normal(k1, (B, C, L), dtype=jnp.float32), 'gate_w': jax.random.normal(k2, (E, L), dtype=jnp.float32) * scale, 'expert_w': jax.random.normal(k3, (E, O, L), dtype=jnp.float32) * scale, 'expert_b': jax.random.normal(k4, (E, O), dtype=jnp.float32) * scale}
    _L0_ffn_all = _L0_ffn_setup()
    _L0_ffn_in = {k: v for k, v in _L0_ffn_all.items() if k in ('gate_w', 'expert_w', 'expert_b')}
    del _L0_ffn_all
    return {'x': x, 'ctx_512': ctx_512, 'g_xattn': g_xattn, 'g_ffn': g_ffn, 'L0_xattn_Wq': _L0_xattn_in['Wq'], 'L0_xattn_Wk': _L0_xattn_in['Wk'], 'L0_xattn_Wv': _L0_xattn_in['Wv'], 'L0_xattn_Wo': _L0_xattn_in['Wo'], 'L0_xattn_bo': _L0_xattn_in['bo'], 'L0_ffn_gate_w': _L0_ffn_in['gate_w'], 'L0_ffn_expert_w': _L0_ffn_in['expert_w'], 'L0_ffn_expert_b': _L0_ffn_in['expert_b']}

def reference(x, ctx_512, g_xattn, g_ffn, L0_xattn_Wq, L0_xattn_Wk, L0_xattn_Wv, L0_xattn_Wo, L0_xattn_bo, L0_ffn_gate_w, L0_ffn_expert_w, L0_ffn_expert_b):
    import jax
    import jax.numpy as jnp

    def _L0_xattn_ref(q, kv, Wq, Wk, Wv, Wo, bo):
        import jax, jax.numpy as jnp
        import numpy as np
        NUM_HEADS = 16
        HEAD_DIM = 64
        Q_DIM = 256
        KV_DIM = 128
        INNER = NUM_HEADS * HEAD_DIM
        B, N, _ = q.shape
        M = kv.shape[1]
        scale = HEAD_DIM ** (-0.5)
        qh = (q @ Wq).reshape(B, N, NUM_HEADS, HEAD_DIM).transpose(0, 2, 1, 3)
        kh = (kv @ Wk).reshape(B, M, NUM_HEADS, HEAD_DIM).transpose(0, 2, 1, 3)
        vh = (kv @ Wv).reshape(B, M, NUM_HEADS, HEAD_DIM).transpose(0, 2, 1, 3)
        scores = jnp.einsum('bhnd,bhmd->bhnm', qh, kh) * scale
        attn = jax.nn.softmax(scores, axis=-1)
        out = jnp.einsum('bhnm,bhmd->bhnd', attn, vh)
        out = out.transpose(0, 2, 1, 3).reshape(B, N, INNER)
        return out @ Wo + bo

    def _L0_ffn_ref(x, gate_w, expert_w, expert_b):
        import jax, jax.numpy as jnp
        import numpy as np
        TOP_K = 2
        N_EXPERTS = 8
        B, C, L = x.shape
        E, O, _ = expert_w.shape
        xt = x.reshape(-1, L)
        router_logits = jnp.einsum('tl,el->te', xt, gate_w)
        probs = jax.nn.softmax(router_logits.astype(jnp.float32), axis=-1)
        routing_weights, selected = jax.lax.top_k(probs, TOP_K)
        comb = jnp.sum(jax.nn.one_hot(selected, E, dtype=routing_weights.dtype) * routing_weights[..., None], axis=1)
        comb = comb.astype(x.dtype)
        out = jnp.zeros((xt.shape[0], O), dtype=x.dtype)
        for e in range(E):
            ye = xt @ expert_w[e].T + expert_b[e]
            out = out + ye * comb[:, e:e + 1]
        return out.reshape(B, C, O)
    x = x + jnp.tanh(g_xattn[0]) * _L0_xattn_ref(_layernorm(x, axis=-1), ctx_512, L0_xattn_Wq, L0_xattn_Wk, L0_xattn_Wv, L0_xattn_Wo, L0_xattn_bo)
    x = x + jnp.tanh(g_ffn[0]) * _L0_ffn_ref(_layernorm(x, axis=-1), L0_ffn_gate_w, L0_ffn_expert_w, L0_ffn_expert_b)
    return x

_drawn_inputs = setup_inputs


def setup_inputs(seed=0):
    import zlib

    import numpy as np

    out = dict(_drawn_inputs(seed))
    spreads = {}
    factors = {}
    for name, (base, spread) in spreads.items():
        noise = np.random.default_rng([zlib.crc32(name.encode()), seed]).standard_normal(out[name].shape)
        drawn = base * np.exp(spread * noise) if base else spread * noise
        out[name] = jnp.asarray(drawn.astype(out[name].dtype))
    for name, factor in factors.items():
        out[name] = (out[name] * factor).astype(out[name].dtype)
    return out
```

```python
import math
from contextlib import ExitStack

import concourse.bass as bass
from concourse import mybir

F32 = mybir.dt.float32
F32R = mybir.dt.float32r
F16 = mybir.dt.float16
ALU = mybir.AluOpType
ACT = mybir.ActivationFunctionType
AX = mybir.AxisListType

P = 128
BATCHES, TOKENS, DIM = 8, 512, 256
CTX, HEADS, HEAD = 128, 16, 64
INNER = HEADS * HEAD
EXPERTS = 8
TT = TOKENS // P
LC = DIM // P
PAIRS = HEADS // 2
HALVES = INNER // 512
EC = EXPERTS * DIM // 512
GROUP = 4
EPS = 1e-5
SCALE = HEAD ** -0.5
P_SHIFT = 7 * math.log(2.0)
V_RANGE = 30000.0

MISC = [("xt", c) for c in range(LC)] + [("v", n) for n in range(TT * HALVES)] + [("q", 0), ("k", 0)]
for _s in range(HEADS):
    if _s % 2 == 0 and _s // 2 + 1 < PAIRS:
        MISC += [("q", _s // 2 + 1), ("k", _s // 2 + 1)]
    if _s % 2 == 1 and _s >= 3:
        MISC += [("ot", (_s - 3) // 2)]
    if _s == 2 * GROUP + 2:
        MISC += [("wo0", t) for t in range(TT)]
MISC += [("ot", PAIRS - 1)] + [("wo1", t) for t in range(TT)]
MISC += [("x2t", c) for c in range(LC)] + [("router", 0)]
MISC += [("expert", t * EC + e) for t in range(TT) for e in range(EC)]
if len(MISC) % 2:
    MISC += [("idle", 0)]
JOB = {name: n for n, name in enumerate(MISC)}
HI = [name for name in MISC if name[0] in ("xt", "v", "q", "k", "ot", "x2t")]
HI_AT = {name: n for n, name in enumerate(HI)}

N_MISC, N_HI = len(MISC), len(HI)
N_MAX = N_ST = HEADS * TT
N_ROW = HEADS + 1 + TT // 2
N_LO = HEADS * 2
DVE_STEPS = 55
POOL_STEPS = 1
ACT_STEPS = 0


def build(nc, x, kv_t, g_xattn, g_ffn, wq, wk, wv, wo, bo, gate_t, expert_t, expert_b, out):
    x_v = x.rearrange("b (t p) d -> p (b t) d", p=P)
    out_v = out.rearrange("b (t p) d -> p (b t) d", p=P)
    kv_v = kv_t.rearrange("b c k -> c b k")

    ctx = ExitStack()
    with ctx:
        def sb(name, shape, dt=F32):
            return ctx.enter_context(nc.sbuf_tensor(name, shape, dt))

        def bank(name):
            return ctx.enter_context(nc.psum_tensor(name, [P, 512], F32))

        def sem(name):
            return ctx.enter_context(nc.semaphore(name))

        wq_s = sb("wq_s", [P, 2, LC, INNER], F32R)
        wk_s = sb("wk_s", [P, 2, INNER], F32R)
        wv_s = sb("wv_s", [P, 2, INNER], F32R)
        wo_s = sb("wo_s", [P, 2, PAIRS, DIM], F32R)
        ex_s = sb("ex_s", [P, 2, LC, EXPERTS * DIM], F32R)
        gt_s = sb("gt_s", [P, 2, LC, EXPERTS], F32R)
        gt_f = sb("gt_f", [P, LC, EXPERTS])
        eb = sb("eb", [EXPERTS, DIM])
        bo_t = sb("bo_t", [P, DIM])
        gates = sb("gates", [P, 2])
        tg = sb("tg", [P, 2])
        ident = sb("ident", [P, P])
        ident_r = sb("ident_r", [P, P], F32R)
        order = sb("order", [P, EXPERTS])
        eps_half = sb("eps_half", [P, 2, TT])
        wv_sum = sb("wv_sum", [P, 8])
        xin = sb("xin", [P, TT, DIM])
        x2 = sb("x2", [P, TT, DIM])
        xn = sb("xn", [P, TT, DIM])
        kvin = sb("kvin", [P, TOKENS])
        kv_s = sb("kv_s", [P, 2, TOKENS], F32R)
        xt_s = sb("xt_s", [P, 2, LC, TOKENS], F32R)
        v_s = sb("v_s", [P, 2, TT, HEADS, HEAD + 1], F16)
        QA = sb("QA", [P, 4, TOKENS], F32R)
        QB = sb("QB", [P, 4, TOKENS], F32R)
        KA = sb("KA", [P, 4, TOKENS], F32R)
        KB = sb("KB", [P, 4, TOKENS], F32R)
        pf = sb("pf", [P, TT, TOKENS])
        p_s = sb("p_s", [P, 2, 2, TT, TOKENS], F16)
        o_n = sb("o_n", [P, 2, TT, P])
        ot_s = sb("ot_s", [P, 2, GROUP, TOKENS], F32R)
        nmax = sb("nmax", [P, 2, TT], F32R)
        stats = sb("stats", [P, TT, 6])
        mv = sb("mv", [P, TT, 2])
        ve = sb("ve", [P, TT])
        rstd = sb("rstd", [P, TT])
        kmax = sb("kmax", [P, 8])
        rden = sb("rden", [P, TT])
        logit = sb("logit", [P, TT, EXPERTS])
        prob = sb("prob", [P, TT, EXPERTS])
        r1 = sb("r1", [P, TT])
        r2 = sb("r2", [P, TT])
        m1 = sb("m1", [P, TT, EXPERTS])
        m2 = sb("m2", [P, TT, EXPERTS])
        w1 = sb("w1", [P, TT, EXPERTS])
        p2 = sb("p2", [P, TT, EXPERTS])
        comb = sb("comb", [P, TT, EXPERTS])
        comb_t = sb("comb_t", [EXPERTS, TOKENS])

        MX = [bank("MX0"), bank("MX1")]
        ST = [bank("ST0"), bank("ST1")]
        MB = [bank("MB0"), bank("MB1")]
        PV = bank("PV")
        ROW = bank("ROW")

        stage = [pf[:, :, :].rearrange("p a b -> p (a b)"),
                 p_s[:, :, :, :, :].rearrange("p a b c d -> p (a b c d)").bitcast(F32)[:, 0:2048],
                 p_s[:, :, :, :, :].rearrange("p a b c d -> p (a b c d)").bitcast(F32)[:, 2048:4096]]

        w_in = [sem(f"w_in{n}") for n in range(5)]
        small_in = sem("small_in")
        w_hi = sem("w_hi")
        w_lo = sem("w_lo")
        setup_pool = sem("setup_pool")
        setup_dve = sem("setup_dve")
        tanh_done = sem("tanh_done")
        x_in, kv_in = sem("x_in"), sem("kv_in")
        x_ln, x_bias = sem("x_ln"), sem("x_bias")
        var_ready, rstd_ready = sem("var_ready"), sem("rstd_ready")
        xn_ready = sem("xn_ready")
        kv_hi, kv_lo = sem("kv_hi"), sem("kv_lo")
        kmax_ready, kmax_all, v_scale = sem("kmax_ready"), sem("kmax_all"), sem("v_scale")
        misc_ready, misc_hi, misc_free = sem("misc_ready"), sem("misc_hi"), sem("misc_free")
        q_dup = [sem("q_dup0"), sem("q_dup1")]
        k_dup = [sem("k_dup0"), sem("k_dup1")]
        max_ready, max_free = sem("max_ready"), sem("max_free")
        row_ready, row_free = sem("row_ready"), sem("row_free")
        st_ready, exp_done = sem("st_ready"), sem("exp_done")
        p_hi_dve, p_hi_act, p_lo = sem("p_hi_dve"), sem("p_hi_act"), sem("p_lo")
        pv_ready, o_ready = sem("pv_ready"), sem("o_ready")
        lg_shift, lg_exp, comb_ready = sem("lg_shift"), sem("lg_exp"), sem("comb_ready")
        y_ready, y_out = sem("y_ready"), sem("y_out")
        dve_step, pool_step = sem("dve_step"), sem("pool_step")
        block = ctx.enter_context(nc.Block())

        def job_at(b, name):
            return b * N_MISC + JOB[name] + 1

        def freed(b, name):
            return b * N_MISC + JOB[name] + 1 + 2

        def hi_at(b, name):
            return b * N_HI + HI_AT[name] + 1

        WEIGHTS = [
            (wq.rearrange("(c p) n -> p c n", p=P), wq_s),
            (wk, wk_s), (wv, wv_s),
            (wo.rearrange("(c p) n -> p c n", p=P), wo_s),
            (expert_t.rearrange("(c p) n -> p c n", p=P), ex_s)]

        def pieces():
            yield 0, wq_s[:, 0, :, :], wq_s[:, 1, :, :], stage[0].rearrange("p (c n) -> p c n", c=LC)
            yield 1, wk_s[:, 0, :], wk_s[:, 1, :], stage[1][:, 0:INNER]
            yield 1, wv_s[:, 0, :], wv_s[:, 1, :], stage[1][:, INNER:2 * INNER]
            yield 2, wo_s[:, 0, :, :], wo_s[:, 1, :, :], stage[2].rearrange("p (c n) -> p c n", c=PAIRS)
            yield 3, ex_s[:, 0, 0, :], ex_s[:, 1, 0, :], stage[0]
            yield 4, ex_s[:, 0, 1, :], ex_s[:, 1, 1, :], stage[1]

        @block.sync
        def _(sp):
            sp.dma_start(stage[0].rearrange("p (c n) -> p c n", c=LC),
                         wq.rearrange("(c p) n -> p c n", p=P)).then_inc(w_in[0], 16)
            sp.dma_start(stage[1][:, 0:INNER], wk).then_inc(w_in[1], 16)
            sp.dma_start(stage[1][:, INNER:2 * INNER], wv).then_inc(w_in[1], 16)
            sp.dma_start(stage[2].rearrange("p (c n) -> p c n", c=PAIRS),
                         wo.rearrange("(c p) n -> p c n", p=P)).then_inc(w_in[2], 16)
            sp.dma_start(gates[:, 0:1], g_xattn.partition_broadcast(P)).then_inc(small_in, 16)
            sp.dma_start(gates[:, 1:2], g_ffn.partition_broadcast(P)).then_inc(small_in, 16)
            sp.dma_start(bo_t[:, :], bo.partition_broadcast(P)).then_inc(small_in, 16)
            sp.dma_start(eb[:, :], expert_b).then_inc(small_in, 16)
            sp.dma_start(gt_f[:, :, :], gate_t.rearrange("(c p) e -> p c e", p=P)).then_inc(small_in, 16)
            sp.wait_ge(w_lo, 1)
            sp.dma_start(stage[0], expert_t[0:P, :]).then_inc(w_in[3], 16)
            sp.wait_ge(w_lo, 3)
            sp.wait_ge(setup_dve, 2)
            sp.dma_start(stage[1], expert_t[P:DIM, :]).then_inc(w_in[4], 16)
            sp.dma_start(xin[:, :, :], x_v[:, 0:TT, :]).then_inc(x_in, 16)
            sp.dma_start(kvin[:, :], kv_v[:, 0, :]).then_inc(kv_in, 16)

            def copies(b, p):
                s = 2 * (p % 2)
                sp.wait_ge(misc_hi, hi_at(b, ("q", p)))
                sp.dma_start(QB[0:HEAD, s:s + 2, :].bitcast(F32), QA[0:HEAD, s:s + 2, :].bitcast(F32)).then_inc(q_dup[p % 2], 16)
                sp.wait_ge(misc_hi, hi_at(b, ("k", p)))
                sp.dma_start(KA[HEAD:P, s:s + 2, :].bitcast(F32), KA[0:HEAD, s:s + 2, :].bitcast(F32)).then_inc(k_dup[p % 2], 16)

            def batch(b, last):
                for p in range(PAIRS):
                    copies(b, p)
                    if p == 1 and not last:
                        sp.wait_ge(x_ln, b + 1)
                        sp.wait_ge(x_bias, b + 1)
                        sp.dma_start(xin[:, :, :], x_v[:, bass.ds(b * TT + TT, TT), :]).then_inc(x_in, 16)
                        sp.wait_ge(kv_hi, b + 1)
                        sp.wait_ge(kv_lo, b + 1)
                        sp.wait_ge(kmax_ready, b + 1)
                        sp.dma_start(kvin[:, :], kv_v[:, bass.ds(b + 1, 1), :].rearrange("c a k -> c (a k)"))\
                          .then_inc(kv_in, 16)
                sp.wait_ge(y_ready, b + 1)
                sp.dma_start(out_v[:, bass.ds(b * TT, TT), :], xn[:, :, :]).then_inc(y_out, 16)

            with sp.Fori(0, BATCHES - 1) as b:
                batch(b, False)
            batch(BATCHES - 1, True)
            sp.wait_ge(y_out, 16 * BATCHES + 16)

        @block.gpsimd
        def _(pool):
            pool.memset(ident[:, :], 0.0).then_inc(setup_pool, 1)
            for e in range(EXPERTS):
                pool.memset(order[:, e:e + 1], float(EXPERTS - e)).then_inc(setup_pool, 1)
            pool.memset(eps_half[:, 0, :], -0.5).then_inc(setup_pool, 1)
            pool.memset(v_s[:, 0, :, :, HEAD:HEAD + 1], 1.0).then_inc(setup_pool, 1)
            pool.memset(v_s[:, 1, :, :, HEAD:HEAD + 1], 0.0).then_inc(setup_pool, 1)
            pool.wait_ge(setup_pool, EXPERTS + 4)
            pool.affine_select(out=ident[:, :], in_=ident[:, :], compare_op=ALU.not_equal, fill=1.0, base=0,
                               pattern=[[-1, P]], channel_multiplier=1).then_inc(setup_pool, 1)
            pool.wait_ge(setup_dve, 2)
            pool.partition_all_reduce(wv_sum[:, 1:2], wv_sum[:, 0:1], P, bass.bass_isa.ReduceOp.add)\
                .then_inc(setup_pool, 1)

            def power(b, n):
                pool.wait_ge(var_ready, 2 * b + n)
                pool.tensor_tensor(rstd[:, :], ve[:, :], eps_half[:, 0, :], ALU.pow).then_inc(rstd_ready, 1)

            with pool.Fori(0, BATCHES) as b:
                pool.wait_ge(setup_dve, 3)
                pool.wait_ge(kmax_ready, b + 1)
                power(b, 1)
                pool.partition_all_reduce(kmax[:, 1:2], kmax[:, 0:1], P, bass.bass_isa.ReduceOp.max)\
                    .then_inc(kmax_all, 1)
                pool.wait_ge(x_in, 16 * b + 16)
                pool.tensor_tensor(x2[:, :, :], xin[:, :, :],
                                   bo_t[:, :].unsqueeze(1).broadcast_to([P, TT, DIM]), ALU.add)\
                    .then_inc(x_bias, 1)
                for h in range(HEADS):
                    for j in range(2):
                        if j == 0:
                            pool.wait_ge(p_hi_dve, b * HEADS + h + 1)
                        else:
                            pool.wait_ge(p_hi_act, b * HEADS + h + 1)
                        t = 2 * j
                        pool.tensor_tensor(p_s[:, h % 2, 1, t:t + 2, :], pf[:, t:t + 2, :],
                                           p_s[:, h % 2, 0, t:t + 2, :], ALU.subtract).then_inc(p_lo, 1)
                power(b, 2)

        @block.scalar
        def _(act):
            for n, (load, hi, lo, raw) in enumerate(pieces()):
                act.wait_ge(w_in[load], 32 if load == 1 else 16)
                act.activation(hi, raw, ACT.Copy).then_inc(w_hi, 1)
            act.wait_ge(small_in, 5 * 16)
            act.activation(gt_s[:, 0, :, :], gt_f[:, :, :], ACT.Copy).then_inc(w_hi, 1)
            act.activation(tg[:, :], gates[:, :], ACT.Tanh).then_inc(tanh_done, 1)

            def take_hi(b, name, pairs):
                act.wait_ge(misc_ready, job_at(b, name))
                for dst, src in pairs[:-1]:
                    act.activation(dst, src, ACT.Copy)
                act.activation(pairs[-1][0], pairs[-1][1], ACT.Copy).then_inc(misc_hi, 1)

            def project(b, p):
                s = 2 * (p % 2)
                for name, dst in (("q", QA), ("k", KA)):
                    m = MB[JOB[(name, p)] % 2]
                    take_hi(b, (name, p), [(dst[0:HEAD, s, :], m[0:HEAD, :]), (dst[0:HEAD, s + 1, :], m[HEAD:P, :])])

            def row(b, h):
                act.wait_ge(row_ready, b * N_ROW + h + 1)
                act.activation(QB[HEAD:HEAD + 1, h % 4, :], ROW[HEAD:HEAD + 1, :], ACT.Copy).then_inc(row_free, 1)

            with act.Fori(0, BATCHES) as b:
                act.wait_ge(kv_in, 16 * b + 16)
                act.activation(kv_s[:, 0, :], kvin[:, :], ACT.Copy).then_inc(kv_hi, 1)
                for c in range(LC):
                    take_hi(b, ("xt", c), [(xt_s[:, 0, c, :], MB[JOB[("xt", c)] % 2][:, :])])
                act.wait_ge(v_scale, b + 1)
                for n in range(TT * HALVES):
                    t, g = divmod(n, HALVES)
                    hs = HEADS // HALVES
                    act.wait_ge(misc_ready, job_at(b, ("v", n)))
                    act.activation(v_s[:, 0, t, g * hs:(g + 1) * hs, 0:HEAD],
                                   MB[JOB[("v", n)] % 2][:, :].rearrange("p (h d) -> p h d", d=HEAD),
                                   ACT.Copy, scale=kmax[:, 3:4]).then_inc(misc_hi, 1)
                project(b, 0)
                row(b, 0)
                for h in range(HEADS):
                    if h % 2 == 0 and h // 2 + 1 < PAIRS:
                        project(b, h // 2 + 1)
                    for t in range(TT):
                        act.wait_ge(st_ready, b * N_ST + h * TT + t + 1)
                        if t % 2 == 0:
                            act.wait_ge(p_lo, b * N_LO + 2 * (h - 1) + t // 2 + 1 + 2)
                        act.activation(pf[:, t, :], ST[t % 2][:, :], ACT.Exp, bias=P_SHIFT, scale=SCALE)\
                           .then_inc(exp_done, 1)
                    if h % 2 == 1 and h >= 3:
                        p = (h - 3) // 2
                        take_hi(b, ("ot", p), [(ot_s[:, 0, p % GROUP, :], MB[JOB[("ot", p)] % 2][:, :])])
                    act.wait_ge(exp_done, b * N_ST + h * TT + TT + 2)
                    act.wait_ge(pv_ready, b * HEADS + h - 1 + 2)
                    act.activation(p_s[:, h % 2, 0, 2:4, :], pf[:, 2:4, :], ACT.Copy).then_inc(p_hi_act, 1)
                    if h + 1 < HEADS:
                        row(b, h + 1)
                p = PAIRS - 1
                take_hi(b, ("ot", p), [(ot_s[:, 0, p % GROUP, :], MB[JOB[("ot", p)] % 2][:, :])])
                for c in range(LC):
                    take_hi(b, ("x2t", c), [(xt_s[:, 0, c, :], MB[JOB[("x2t", c)] % 2][:, :])])
                act.wait_ge(lg_shift, b + 1)
                act.activation(prob[:, :, :], logit[:, :, :], ACT.Exp).then_inc(lg_exp, 1)
                act.wait_ge(row_ready, b * N_ROW + HEADS + 1)
                act.activation(comb_t[:, :], ROW[0:EXPERTS, :], ACT.Copy).then_inc(row_free, 1)
                for j in range(TT // 2):
                    act.wait_ge(row_ready, b * N_ROW + HEADS + 2 + j)
                    act.activation(xn[:, 2 * j:2 * j + 2, :], ROW[:, :].rearrange("p (a n) -> p a n", a=2), ACT.Copy)\
                       .then_inc(row_free, 1)

        @block.vector
        def _(dve):
            dve.memset(kmax[:, :], 0.0).then_inc(misc_free, 2)
            dve.memset(rden[:, :], 0.0).then_inc(max_free, 2)
            dve.memset(r1[:, :], 0.0).then_inc(row_free, 1)
            dve.memset(r2[:, :], 0.0).then_inc(exp_done, 2)
            dve.memset(ve[:, :], 0.0).then_inc(p_lo, 2)
            dve.memset(rstd[:, :], 0.0).then_inc(pv_ready, 2)
            dve.memset(mv[:, :, :], 0.0).then_inc(o_ready, 1)
            dve.memset(stats[:, :, :], 0.0).then_inc(y_out, 16)
            dve.memset(KB[HEAD:HEAD + 1, :, :].bitcast(F32), 1.0).then_inc(setup_dve, 1)
            for n, (load, hi, lo, raw) in enumerate(pieces()):
                dve.wait_ge(w_hi, n + 1)
                dve.tensor_tensor(lo, raw, hi.bitcast(F32), ALU.subtract).then_inc(w_lo, 1)
                if n == 2:
                    dve.tensor_reduce(wv_sum[:, 0:1], raw, AX.X, ALU.max, apply_absolute_value=True)\
                       .then_inc(setup_dve, 1)
            dve.wait_ge(w_hi, 7)
            dve.tensor_tensor(gt_s[:, 1, :, :], gt_f[:, :, :], gt_s[:, 0, :, :].bitcast(F32), ALU.subtract)\
               .then_inc(w_lo, 1)
            dve.wait_ge(tanh_done, 1)
            dve.tensor_scalar(bo_t[:, :], bo_t[:, :], tg[:, 0:1], None, ALU.mult).then_inc(setup_dve, 1)
            dve.wait_ge(setup_pool, EXPERTS + 5)
            dve.tensor_copy(ident_r[:, :], ident[:, :]).then_inc(setup_dve, 1)
            dve.wait_ge(setup_dve, 4)
            dve.wait_ge(w_lo, 7)

            with dve.Fori(0, BATCHES) as b:
                chain = [0]

                def step(ins):
                    chain[0] += 1
                    ins.then_inc(dve_step, 1)
                    dve.wait_ge(dve_step, b * DVE_STEPS + chain[0])

                def layernorm(src, n, read):
                    for t in range(TT):
                        last = dve.bn_stats(stats[:, t, :], src[:, t, :])
                    step(last)
                    dve.memset(ve[:, :], 0.0)
                    for t in range(TT):
                        last = dve.bn_aggr(mv[:, t, :], stats[:, t, :])
                    step(last)
                    dve.tensor_scalar(ve[:, :], mv[:, :, 1], EPS, None, ALU.add).then_inc(var_ready, 1)
                    dve.wait_ge(rstd_ready, 2 * b + n)
                    for t in range(TT):
                        last = dve.tensor_scalar(xn[:, t, :], src[:, t, :], mv[:, t, 0:1], rstd[:, t:t + 1],
                                                 ALU.subtract, ALU.mult)
                    last.then_inc(read, 1)

                def take_lo(name, triples):
                    dve.wait_ge(misc_hi, hi_at(b, name))
                    for dst, src, hi in triples[:-1]:
                        dve.tensor_tensor(dst, src, hi.bitcast(F32), ALU.subtract)
                    dst, src, hi = triples[-1]
                    dve.tensor_tensor(dst, src, hi.bitcast(F32), ALU.subtract).then_inc(misc_free, 1)

                def project(p):
                    s = 2 * (p % 2)
                    m = MB[JOB[("q", p)] % 2]
                    take_lo(("q", p), [(QA[HEAD:P, s + i, :], m[HEAD * i:HEAD * i + HEAD, :], QA[0:HEAD, s + i, :])
                                       for i in range(2)])
                    m = MB[JOB[("k", p)] % 2]
                    take_lo(("k", p), [(KB[0:HEAD, s + i, :], m[HEAD * i:HEAD * i + HEAD, :], KA[0:HEAD, s + i, :])
                                       for i in range(2)])

                def maxima(h, ts):
                    for t in ts:
                        dve.wait_ge(max_ready, b * N_MAX + h * TT + t + 1)
                        dve.tensor_reduce(nmax[:, h % 2, t:t + 1], MX[t % 2][:, :], AX.X, ALU.max, negate=True)\
                           .then_inc(max_free, 1)

                def normalise(h):
                    dve.wait_ge(pv_ready, b * HEADS + h + 1 + 2)
                    acc = PV[:, 0:TT * (HEAD + 1)].rearrange("p (t d) -> p t d", t=TT)
                    step(dve.reciprocal(rden[:, :], acc[:, :, HEAD]))
                    if h % 2 == 0 and h >= 4:
                        dve.wait_ge(misc_ready, job_at(b, ("ot", h // 2 - 2)))
                    dve.scalar_tensor_tensor(o_n[:, h // 2 % 2, :, HEAD * (h % 2):HEAD * (h % 2) + HEAD],
                                             acc[:, :, 0:HEAD], kmax[:, 4:5],
                                             rden[:, :].unsqueeze(2).broadcast_to([P, TT, HEAD]),
                                             ALU.mult, ALU.mult).then_inc(o_ready, 1)

                def turned(p):
                    m = MB[JOB[("ot", p)] % 2]
                    take_lo(("ot", p), [(ot_s[:, 1, p % GROUP, :], m[:, :], ot_s[:, 0, p % GROUP, :])])

                def add_attention(half):
                    for t in range(TT):
                        dve.wait_ge(misc_ready, job_at(b, (f"wo{half}", t)))
                        dve.scalar_tensor_tensor(x2[:, t, :], MB[JOB[(f"wo{half}", t)] % 2][:, 0:DIM], tg[:, 0:1],
                                                 x2[:, t, :], ALU.mult, ALU.add).then_inc(misc_free, 1)

                dve.wait_ge(kv_in, 16 * b + 16)
                dve.wait_ge(kv_hi, b + 1)
                dve.tensor_tensor(kv_s[:, 1, :], kvin[:, :], kv_s[:, 0, :].bitcast(F32), ALU.subtract)\
                   .then_inc(kv_lo, 1)
                dve.tensor_reduce(kmax[:, 0:1], kvin[:, :], AX.X, ALU.max, apply_absolute_value=True)\
                   .then_inc(kmax_ready, 1)
                dve.wait_ge(x_in, 16 * b + 16)
                dve.wait_ge(y_out, 16 * b + 16)
                layernorm(xin, 1, x_ln)
                for c in range(LC):
                    take_lo(("xt", c), [(xt_s[:, 1, c, :], MB[JOB[("xt", c)] % 2][:, :], xt_s[:, 0, c, :])])
                dve.wait_ge(kmax_all, b + 1)
                dve.wait_ge(setup_pool, EXPERTS + 6)
                step(dve.tensor_scalar(kmax[:, 4:5], kmax[:, 1:2], wv_sum[:, 1:2], 1.0 / V_RANGE, ALU.mult, ALU.mult))
                step(dve.tensor_scalar(kmax[:, 4:5], kmax[:, 4:5], 1e-30, None, ALU.max))
                dve.reciprocal(kmax[:, 3:4], kmax[:, 4:5]).then_inc(v_scale, 1)
                dve.wait_ge(v_scale, b + 1)
                hs = HEADS // HALVES
                for n in range(TT * HALVES):
                    t, g = divmod(n, HALVES)
                    dve.wait_ge(misc_hi, hi_at(b, ("v", n)))
                    dve.scalar_tensor_tensor(v_s[:, 1, t, g * hs:(g + 1) * hs, 0:HEAD],
                                             MB[JOB[("v", n)] % 2][:, :].rearrange("p (h d) -> p h d", d=HEAD),
                                             kmax[:, 3:4], v_s[:, 0, t, g * hs:(g + 1) * hs, 0:HEAD],
                                             ALU.mult, ALU.subtract).then_inc(misc_free, 1)
                project(0)
                maxima(0, range(TT))
                for h in range(HEADS):
                    if h % 2 == 0 and h // 2 + 1 < PAIRS:
                        project(h // 2 + 1)
                    if h + 1 < HEADS:
                        maxima(h + 1, (0, 1))
                    dve.wait_ge(exp_done, b * N_ST + h * TT + 2 + 2)
                    dve.wait_ge(pv_ready, b * HEADS + h - 1 + 2)
                    dve.tensor_copy(p_s[:, h % 2, 0, 0:2, :], pf[:, 0:2, :]).then_inc(p_hi_dve, 1)
                    if h + 1 < HEADS:
                        maxima(h + 1, (2, 3))
                    if h % 2 == 1 and h >= 3:
                        turned((h - 3) // 2)
                    if h == 2 * GROUP + 2:
                        dve.wait_ge(x_bias, b + 1)
                        add_attention(0)
                    if h >= 1:
                        normalise(h - 1)
                normalise(HEADS - 1)
                turned(PAIRS - 1)
                dve.wait_ge(misc_free, freed(b, ("wo0", TT - 1)))
                add_attention(1)
                dve.wait_ge(misc_free, freed(b, ("wo1", TT - 1)))
                layernorm(x2, 2, xn_ready)
                for c in range(LC):
                    take_lo(("x2t", c), [(xt_s[:, 1, c, :], MB[JOB[("x2t", c)] % 2][:, :], xt_s[:, 0, c, :])])
                dve.wait_ge(misc_ready, job_at(b, ("router", 0)))
                step(dve.tensor_copy(m1[:, :, :], MB[JOB[("router", 0)] % 2][:, 0:TT * EXPERTS]
                                     .rearrange("p (t e) -> p t e", t=TT)))

                def over(v):
                    return v[:, :].unsqueeze(2).broadcast_to([P, TT, EXPERTS])

                order_b = order[:, :].unsqueeze(1).broadcast_to([P, TT, EXPERTS])
                step(dve.tensor_reduce(r1[:, :], m1[:, :, :], AX.X, ALU.max, negate=True))
                dve.tensor_tensor(logit[:, :, :], m1[:, :, :], over(r1), ALU.add).then_inc(lg_shift, 1)
                dve.wait_ge(lg_exp, b + 1)
                step(dve.tensor_reduce(r1[:, :], prob[:, :, :], AX.X, ALU.add))
                step(dve.reciprocal(r2[:, :], r1[:, :]))
                step(dve.tensor_tensor(prob[:, :, :], prob[:, :, :], over(r2), ALU.mult))

                def first_largest(mask, src):
                    step(dve.tensor_reduce(r1[:, :], src[:, :, :], AX.X, ALU.max))
                    step(dve.tensor_tensor(w1[:, :, :], src[:, :, :], over(r1), ALU.is_equal))
                    step(dve.tensor_tensor(w1[:, :, :], w1[:, :, :], order_b, ALU.mult))
                    step(dve.tensor_reduce(r1[:, :], w1[:, :, :], AX.X, ALU.max))
                    step(dve.tensor_tensor(mask[:, :, :], w1[:, :, :], over(r1), ALU.is_equal))

                first_largest(m1, prob)
                step(dve.scalar_tensor_tensor(p2[:, :, :], m1[:, :, :], -2.0, prob[:, :, :], ALU.mult, ALU.add))
                first_largest(m2, p2)
                step(dve.tensor_tensor(m2[:, :, :], m1[:, :, :], m2[:, :, :], ALU.add))
                dve.tensor_tensor(comb[:, :, :], prob[:, :, :], m2[:, :, :], ALU.mult).then_inc(comb_ready, 1)
                dve.wait_ge(comb_ready, b + 1)
                dve.memset(w1[:, 0, 0:1], 0.0).then_inc(misc_free, 1)
                for t in range(TT):
                    dve.wait_ge(row_free, b * N_ROW + HEADS + 2 + t // 2 + 1)
                    for n in range(EXPERTS):
                        name = ("expert", t * EC + n // 2)
                        if n % 2 == 0:
                            dve.wait_ge(misc_ready, job_at(b, name))
                        ins = dve.scalar_tensor_tensor(xn[:, t, :],
                                                       MB[JOB[name] % 2][:, DIM * (n % 2):DIM * (n % 2) + DIM],
                                                       comb[:, t, n:n + 1], xn[:, t, :], ALU.mult, ALU.add)
                        if n % 2 == 0:
                            step(ins)
                        else:
                            ins.then_inc(misc_free, 1)
                            dve.wait_ge(misc_free, freed(b, name))
                last = dve.scalar_tensor_tensor(xn[:, :, :], xn[:, :, :], tg[:, 1:2], x2[:, :, :],
                                                ALU.mult, ALU.add)
                last.then_inc(y_ready, 1)
                if ("idle", 0) in JOB:
                    dve.memset(r1[:, :], 0.0).then_inc(misc_free, 1)
                assert chain[0] == DVE_STEPS, chain[0]

        @block.tensor
        def _(pe):
            pe.wait_ge(setup_pool, EXPERTS + 5)
            pe.wait_ge(setup_dve, 4)
            pe.wait_ge(w_lo, 7)

            with pe.Fori(0, BATCHES) as b:
                def begin(name):
                    pe.wait_ge(misc_free, b * N_MISC + JOB[name] + 1)
                    return MB[JOB[name] % 2]

                def parts(dst, terms):
                    n = 3 * len(terms)
                    k = 0
                    for (s_hi, s_lo), (m_hi, m_lo) in terms:
                        for s, m in ((s_hi, m_hi), (s_hi, m_lo), (s_lo, m_hi)):
                            last = pe.matmul(dst, s, m, start=(k == 0), stop=(k == n - 1))
                            k += 1
                    return last

                def turn_x(name, c):
                    m = begin((name, c))
                    for t in range(TT):
                        last = pe.transpose(m[:, t * P:(t + 1) * P], xn[:, t, c * P:(c + 1) * P], ident[:, :])
                    last.then_inc(misc_ready, 1)

                def project(p):
                    cols = slice(p * P, (p + 1) * P)
                    parts(begin(("q", p))[:, :],
                          [((wq_s[:, 0, c, cols], wq_s[:, 1, c, cols]), (xt_s[:, 0, c, :], xt_s[:, 1, c, :]))
                           for c in range(LC)]).then_inc(misc_ready, 1)
                    parts(begin(("k", p))[:, :],
                          [((wk_s[:, 0, cols], wk_s[:, 1, cols]), (kv_s[:, 0, :], kv_s[:, 1, :]))])\
                        .then_inc(misc_ready, 1)

                def maxima(h, ts):
                    for t in ts:
                        pe.wait_ge(max_free, b * N_MAX + h * TT + t + 1)
                        pe.matmul(MX[t % 2][:, :], QA[0:HEAD, h % 4, t * P:(t + 1) * P], KA[0:HEAD, h % 4, :],
                                  start=True, stop=True).then_inc(max_ready, 1)

                def row(h):
                    pe.wait_ge(max_free, b * N_MAX + (h + 1) * TT + 2)
                    pe.wait_ge(row_free, b * N_ROW + h + 1)
                    for t in range(TT):
                        last = pe.matmul(ROW[:, t * P:(t + 1) * P], nmax[:, h % 2, t:t + 1].broadcast_to([P, P]),
                                         ident_r[:, :], start=True, stop=True)
                    last.then_inc(row_ready, 1)

                def scores(h, t):
                    s = h % 4
                    pe.wait_ge(exp_done, b * N_ST + h * TT + t + 1)
                    pe.matmul(ST[t % 2][:, :], KA[:, s, t * P:(t + 1) * P], QA[:, s, :], start=True, stop=False)
                    pe.matmul(ST[t % 2][:, :], KB[0:HEAD + 1, s, t * P:(t + 1) * P], QB[0:HEAD + 1, s, :],
                              start=False, stop=True).then_inc(st_ready, 1)

                def values(h, ts):
                    for t in ts:
                        for k in range(TT):
                            for n, (i, j) in enumerate(((0, 0), (0, 1), (1, 0))):
                                last = pe.matmul(PV[:, t * (HEAD + 1):(t + 1) * (HEAD + 1)],
                                                 p_s[:, h % 2, i, k, t * P:(t + 1) * P], v_s[:, j, k, h, :],
                                                 start=(k == 0 and n == 0), stop=(k == TT - 1 and n == 2))
                    if TT - 1 in ts:
                        last.then_inc(pv_ready, 1)

                def turn_o(p):
                    m = begin(("ot", p))
                    pe.wait_ge(o_ready, b * HEADS + 2 * p + 2 + 1)
                    for t in range(TT):
                        last = pe.transpose(m[:, t * P:(t + 1) * P], o_n[:, p % 2, t, :], ident[:, :])
                    last.then_inc(misc_ready, 1)

                def output(half):
                    pe.wait_ge(misc_free, freed(b, ("ot", half * GROUP + GROUP - 1)))
                    for t in range(TT):
                        q = slice(t * P, (t + 1) * P)
                        parts(begin((f"wo{half}", t))[:, 0:DIM],
                              [((ot_s[:, 0, j, q], ot_s[:, 1, j, q]),
                                (wo_s[:, 0, half * GROUP + j, :], wo_s[:, 1, half * GROUP + j, :]))
                               for j in range(GROUP)]).then_inc(misc_ready, 1)

                pe.wait_ge(x_ln, b + 1)
                for c in range(LC):
                    turn_x("xt", c)
                pe.wait_ge(kv_lo, b + 1)
                for n in range(TT * HALVES):
                    t, g = divmod(n, HALVES)
                    q, cols = slice(t * P, (t + 1) * P), slice(g * 512, (g + 1) * 512)
                    parts(begin(("v", n))[:, :], [((kv_s[:, 0, q], kv_s[:, 1, q]),
                                                   (wv_s[:, 0, cols], wv_s[:, 1, cols]))]).then_inc(misc_ready, 1)
                pe.wait_ge(misc_free, freed(b, ("xt", LC - 1)))
                project(0)
                pe.wait_ge(misc_hi, hi_at(b, ("k", 0)))
                maxima(0, range(TT))
                row(0)
                for h in range(HEADS):
                    p = h // 2
                    if h % 2 == 0:
                        if p + 1 < PAIRS:
                            project(p + 1)
                        pe.wait_ge(misc_free, freed(b, ("k", p)))
                        pe.wait_ge(q_dup[p % 2], 16 * (b * (PAIRS // 2) + p // 2 + 1))
                        pe.wait_ge(k_dup[p % 2], 16 * (b * (PAIRS // 2) + p // 2 + 1))
                    pe.wait_ge(row_free, b * N_ROW + h + 1 + 1)
                    scores(h, 0)
                    scores(h, 1)
                    if h + 1 < HEADS:
                        if h % 2 == 1:
                            pe.wait_ge(misc_hi, hi_at(b, ("k", p + 1)))
                        maxima(h + 1, (0, 1))
                    scores(h, 2)
                    if h >= 1:
                        pe.wait_ge(p_lo, b * N_LO + 2 * h + 2)
                        pe.wait_ge(o_ready, b * HEADS + h - 1 + 1)
                        values(h - 1, (0, 1))
                    scores(h, 3)
                    if h + 1 < HEADS:
                        maxima(h + 1, (2, 3))
                    if h >= 1:
                        values(h - 1, (2, 3))
                    if h % 2 == 1 and h >= 3:
                        turn_o((h - 3) // 2)
                    if h + 1 < HEADS:
                        row(h + 1)
                    if h == 2 * GROUP + 2:
                        output(0)
                pe.wait_ge(p_lo, b * N_LO + 2 * HEADS + 2)
                pe.wait_ge(o_ready, b * HEADS + HEADS - 1 + 1)
                values(HEADS - 1, range(TT))
                turn_o(PAIRS - 1)
                output(1)
                pe.wait_ge(xn_ready, b + 1)
                for c in range(LC):
                    turn_x("x2t", c)
                pe.wait_ge(misc_free, freed(b, ("x2t", LC - 1)))
                m = begin(("router", 0))
                for t in range(TT):
                    q = slice(t * P, (t + 1) * P)
                    last = parts(m[:, t * EXPERTS:(t + 1) * EXPERTS],
                                 [((xt_s[:, 0, c, q], xt_s[:, 1, c, q]), (gt_s[:, 0, c, :], gt_s[:, 1, c, :]))
                                  for c in range(LC)])
                last.then_inc(misc_ready, 1)
                for t in range(TT):
                    q = slice(t * P, (t + 1) * P)
                    if t == 1:
                        pass
                    for e in range(EC):
                        cols = slice(e * 512, (e + 1) * 512)
                        parts(begin(("expert", t * EC + e))[:, :],
                              [((xt_s[:, 0, c, q], xt_s[:, 1, c, q]), (ex_s[:, 0, c, cols], ex_s[:, 1, c, cols]))
                               for c in range(LC)]).then_inc(misc_ready, 1)
                        if t == 0 and e == 0:
                            pe.wait_ge(comb_ready, b + 1)
                            pe.wait_ge(row_free, b * N_ROW + HEADS + 1)
                            for u in range(TT):
                                last = pe.transpose(ROW[0:EXPERTS, u * P:(u + 1) * P], comb[:, u, :], ident[:, :])
                            last.then_inc(row_ready, 1)
                            for j in range(TT // 2):
                                pe.wait_ge(row_free, b * N_ROW + HEADS + 2 + j)
                                for u in (0, 1):
                                    k = 2 * j + u
                                    last = pe.matmul(ROW[:, u * DIM:(u + 1) * DIM], comb_t[:, k * P:(k + 1) * P],
                                                     eb[:, :], start=True, stop=True)
                                last.then_inc(row_ready, 1)
                if ("idle", 0) in JOB:
                    pe.wait_ge(misc_free, b * N_MISC + JOB[("idle", 0)] + 1)
                    pe.transpose(MB[JOB[("idle", 0)] % 2][:, 0:P], ident[:, :], ident[:, :]).then_inc(misc_ready, 1)


def kernel(x, ctx_512, g_xattn, g_ffn, L0_xattn_Wq, L0_xattn_Wk, L0_xattn_Wv, L0_xattn_Wo, L0_xattn_bo,
           L0_ffn_gate_w, L0_ffn_expert_w, L0_ffn_expert_b):
    import numpy as np
    import concourse.bacc as bacc
    from concourse.bass_utils import run_bass_kernel_spmd

    nc = bacc.Bacc("TRN2", target_bir_lowering=False, num_devices=1)
    ins = {
        "x": x,
        "kv_t": np.asarray(ctx_512).transpose(0, 2, 1),
        "g_xattn": g_xattn,
        "g_ffn": g_ffn,
        "wq": L0_xattn_Wq, "wk": L0_xattn_Wk, "wv": L0_xattn_Wv, "wo": L0_xattn_Wo, "bo": L0_xattn_bo,
        "gate_t": np.asarray(L0_ffn_gate_w).T,
        "expert_t": np.asarray(L0_ffn_expert_w).transpose(2, 0, 1).reshape(DIM, EXPERTS * DIM),
        "expert_b": L0_ffn_expert_b,
    }
    ins = {n: np.ascontiguousarray(a) for n, a in ins.items()}
    aps = {n: nc.dram_tensor(n, a.shape, mybir.dt.from_np(a.dtype), kind="ExternalInput").ap()
           for n, a in ins.items()}
    out = nc.dram_tensor("out", (BATCHES, TOKENS, DIM), F32, kind="ExternalOutput").ap()
    build(nc, out=out, **aps)
    r = run_bass_kernel_spmd(nc, [ins], core_ids=[0])
    return r.results[0]["out"]
```

```python
import math
from contextlib import ExitStack

import concourse.bass as bass
from concourse import mybir

F32 = mybir.dt.float32
F32R = mybir.dt.float32r
F16 = mybir.dt.float16
ALU = mybir.AluOpType
ACT = mybir.ActivationFunctionType
AX = mybir.AxisListType

P = 128
BATCHES, TOKENS, DIM = 8, 512, 256
CTX, HEADS, HEAD = 128, 16, 64
INNER = HEADS * HEAD
EXPERTS = 8
TT = TOKENS // P
LC = DIM // P
PAIRS = HEADS // 2
HALVES = INNER // 512
EC = EXPERTS * DIM // 512
GROUP = 2
EPS = 1e-5
SCALE = HEAD ** -0.5
P_SHIFT = 7 * math.log(2.0)
V_RANGE = 30000.0

ROUNDS = PAIRS // GROUP
MT = TT // 2
HH = HEADS // HALVES

PRO, FIRST, LOOP, LAST, EPI = "pro", "first", "loop", "last", "epi"


def jobs_of(kind, h, t):
    jobs = []
    if h % 2 == 0 and t == 0:
        jobs.append(("k", (h + 2) // 2 % PAIRS))
    if h % 2 and t == TT - 1:
        jobs.append(("q", (h + 3) // 2 % PAIRS))
    if h % 2 and t == 2:
        jobs.append(("ot", (h - 3) // 2 % PAIRS))
    if h % 4 == 2 and t in (1, 3):
        jobs.append(("wo", (h - 6) // 4 % ROUNDS, t // 2))
    jobs += PLACED.get((h, t), [])
    absent = {FIRST: [("ot", PAIRS - 1)] + [("wo", ROUNDS - 1, j) for j in range(MT)] + EXPERT_JOBS,
              LOOP: [], LAST: NEXT_JOBS}[kind]
    return [name for name in jobs if name not in absent]


NEXT_JOBS = [("xt", 0), ("xt", 1), ("bound",), ("q", 0), ("k", 0)] + [("v", t, 0) for t in range(TT)] + [("q", 1)]
PLACED = {
    (1, 1): [("v", 0, 1)], (2, 2): [("v", 1, 1)], (4, 2): [("v", 2, 1)], (6, 2): [("v", 3, 1)],
    (4, 1): [("x2t", 0)], (4, 3): [("x2t", 1)], (5, 1): [("router",)], (6, 0): [("logits",)],
    (8, 1): [("gates",), ("expert", 0, 0)], (8, 2): [("expert", 0, 1)], (8, 3): [("bias", 0), ("bias", 1)],
    (9, 2): [("bound",)], (12, 1): [("xt", 0)], (12, 2): [("xt", 1)],
    (14, 2): [("v", 0, 0)], (15, 0): [("v", 1, 0)], (15, 1): [("v", 2, 0)], (15, 2): [("v", 3, 0)],
}
for _n in range(2, TT * EC):
    _h = 8 + _n // 2
    PLACED.setdefault((_h, (_n % 2) if _h % 2 else 3 * (_n % 2)), []).append(("expert", _n // EC, _n % EC))
SUMMED = [name for _at in sorted(PLACED) for name in PLACED[_at] if name[0] in ("bias", "expert")]
EXPERT_JOBS = [name for _at in sorted(PLACED) for name in PLACED[_at]
               if name[0] in ("x2t", "router", "logits", "gates", "bias", "expert")]

JOBS = {PRO: NEXT_JOBS, EPI: [("ot", PAIRS - 1)] + [("wo", ROUNDS - 1, j) for j in range(MT)] + EXPERT_JOBS}
for _kind in (FIRST, LOOP, LAST):
    JOBS[_kind] = [name for _h in range(HEADS) for _t in range(TT) for name in jobs_of(_kind, _h, _t)]
SPLIT = ("q", "k", "v", "xt", "ot", "x2t")
HI = {kind: [n for n in names if n[0] in SPLIT] for kind, names in JOBS.items()}
BANKS = 3
assert len(JOBS[LOOP]) % BANKS == 0

VALUES_SLOTS = {3: (1, 0), 0: (2, 1)}
ROW_UNIT = 3
LOGITS_AT = (6, 2)
ROUTE_SLOTS = [(6, 3), (7, 0), (7, 1), (7, 2), (7, 3), (8, 0)]


def maximum_at(kind, h, t):
    g, u = (h + 1, t + TT // 2) if t < TT // 2 else (h + 2, t - TT // 2)
    return (g, u) if g < HEADS or kind != LAST else None


def taken_in(kind, h, t):
    names = jobs_of(kind, *((h, t - 1) if t else (h - 1, TT - 1))) if (h, t) != (0, 0) else []
    return names + (jobs_of(kind, h, t) if (h, t) == (HEADS - 1, TT - 1) else [])


class Iteration:

    def __init__(self, kind, b):
        self.kind, self.b = kind, b

    def start(self, lists):
        n = {kind: len(names) for kind, names in lists.items()}
        return {PRO: 0, FIRST: n[PRO], LOOP: (self.b - 1) * n[LOOP] + (n[PRO] + n[FIRST]),
                LAST: n[PRO] + n[FIRST] + (BATCHES - 2) * n[LOOP],
                EPI: n[PRO] + n[FIRST] + (BATCHES - 2) * n[LOOP] + n[LAST]}[self.kind]

    def done(self, lists, name):
        return self.start(lists) + (lists[self.kind].index(name) + 1)

    def done_before(self, lists, name):
        before = {FIRST: PRO, LOOP: LOOP, LAST: LOOP, EPI: LAST}[self.kind]
        return self.start(lists) - (len(lists[before]) - lists[before].index(name) - 1)

    def bank(self, name):
        start = len(JOBS[PRO]) + len(JOBS[FIRST]) if self.kind == LOOP else self.start(JOBS)
        return (start + JOBS[self.kind].index(name)) % BANKS


def build(nc, x, kv_t, g_xattn, g_ffn, wq, wk, wv, wo, bo, gate_t, expert_t, expert_b, out):
    x_v = x.rearrange("b (t p) d -> p (b t) d", p=P)
    out_v = out.rearrange("b (t p) d -> p (b t) d", p=P)
    kv_v = kv_t.rearrange("b c k -> c b k")

    ctx = ExitStack()
    with ctx:
        def sb(name, shape, dt=F32):
            return ctx.enter_context(nc.sbuf_tensor(name, shape, dt))

        def bank(name):
            return ctx.enter_context(nc.psum_tensor(name, [P, 512], F32))

        def sem(name):
            return ctx.enter_context(nc.semaphore(name))

        wq_s = sb("wq_s", [P, 2, LC, INNER], F32R)
        wk_s = sb("wk_s", [P, 2, INNER], F32R)
        wv_s = sb("wv_s", [P, 2, INNER], F32R)
        wo_s = sb("wo_s", [P, 2, PAIRS, DIM], F32R)
        ex_s = sb("ex_s", [P, 2, LC, EXPERTS * DIM], F32R)
        gt_s = sb("gt_s", [P, 2, LC, EXPERTS], F32R)
        gt_f = sb("gt_f", [P, LC, EXPERTS])
        eb = sb("eb", [EXPERTS, DIM])
        bo_t = sb("bo_t", [P, DIM])
        gates = sb("gates", [P, 2])
        tg = sb("tg", [P, 2])
        ident = sb("ident", [P, P])
        ident_r = sb("ident_r", [P, P], F32R)
        order = sb("order", [P, EXPERTS])
        minus_half = sb("minus_half", [P, TT])
        ones = sb("ones", [P, 1])
        wv_max = sb("wv_max", [P, 1])
        xin = sb("xin", [P, TT, DIM])
        x2 = sb("x2", [P, TT, DIM])
        xn = sb("xn", [P, TT, DIM])
        kvin = sb("kvin", [P, TOKENS])
        kv_s = sb("kv_s", [P, 2, TOKENS], F32R)
        xt_s = sb("xt_s", [P, 2, LC, TOKENS], F32R)
        v_s = sb("v_s", [P, 2, TT, HEADS, HEAD + 1], F16)
        QA = sb("QA", [P, 4, TOKENS], F32R)
        QB = sb("QB", [P, 4, TOKENS], F32R)
        KA = sb("KA", [P, 4, TOKENS], F32R)
        KB = sb("KB", [P, 4, TOKENS], F32R)
        pf = sb("pf", [P, TT, TOKENS])
        p_s = sb("p_s", [P, 2, 2, TT, TOKENS], F16)
        o_n = sb("o_n", [P, 2, TT, P])
        ot_s = sb("ot_s", [P, 2, GROUP, TOKENS], F32R)
        nmax = sb("nmax", [P, 2, TT], F32R)
        stats = sb("stats", [P, TT, 6])
        mv = sb("mv", [P, TT, 2])
        ve = sb("ve", [P, TT])
        rstd = sb("rstd", [P, TT])
        kmax = sb("kmax", [P, 2])
        v_div = sb("v_div", [P, 1])
        v_mul = sb("v_mul", [P, 1])
        o_mul = sb("o_mul", [P, 1])
        rden = sb("rden", [P, TT])
        x2t_s = sb("x2t_s", [P, 2, LC, TOKENS], F32R)
        acc = sb("acc", [P, TT, DIM])
        logit = sb("logit", [P, TT, EXPERTS])
        prob = sb("prob", [P, TT, EXPERTS])
        r1 = sb("r1", [P, TT])
        r2 = sb("r2", [P, TT])
        m1 = sb("m1", [P, TT, EXPERTS])
        m2 = sb("m2", [P, TT, EXPERTS])
        w1 = sb("w1", [P, TT, EXPERTS])
        p2 = sb("p2", [P, TT, EXPERTS])
        comb = sb("comb", [P, TT, EXPERTS])
        comb_t = xn[0:EXPERTS, :, :].rearrange("p t d -> p (t d)")[:, 0:TOKENS]

        MX = [bank("MX0"), bank("MX1")]
        ST = [bank("ST0"), bank("ST1")]
        MB = [bank(f"MB{n}") for n in range(BANKS)]
        PV = bank("PV")

        flat = p_s[:, :, :, :, :].rearrange("p a b c d -> p (a b c d)").bitcast(F32)
        stage_q = pf[:, :, :].rearrange("p a b -> p (a b)")
        stage_k, stage_v = flat[:, 0:INNER], flat[:, INNER:2 * INNER]
        late_stage = acc[:, :, :].rearrange("p t d -> p (t d)")

        wq_in, wk_in, wv_in, small_in = sem("wq_in"), sem("wk_in"), sem("wv_in"), sem("small_in")
        late_in = sem("late_in")
        w_hi, w_lo = sem("w_hi"), sem("w_lo")
        late_hi, late_lo = sem("late_hi"), sem("late_lo")
        const_pool, const_dve = sem("const_pool"), sem("const_dve")
        tanh_done = sem("tanh_done")
        x_in, kv_in = sem("x_in"), sem("kv_in")
        x_bias = sem("x_bias")
        ln1_step, ln1_var, ln1_rstd, ln1_done = sem("ln1_step"), sem("ln1_var"), sem("ln1_rstd"), sem("ln1_done")
        ln2_step, ln2_var, ln2_rstd, ln2_done = sem("ln2_step"), sem("ln2_var"), sem("ln2_rstd"), sem("ln2_done")
        kv_hi, kv_lo = sem("kv_hi"), sem("kv_lo")
        kmax_step, kmax_done = sem("kmax_step"), sem("kmax_done")
        scale_done, o_mul_done = sem("scale_done"), sem("o_mul_done")
        job_ready, job_hi, job_free = sem("job_ready"), sem("job_hi"), sem("job_free")
        q_dup = [sem("q_dup0"), sem("q_dup1")]
        k_dup = [sem("k_dup0"), sem("k_dup1")]
        max_ready, max_free = sem("max_ready"), sem("max_free")
        st_ready, st_free = sem("st_ready"), sem("st_free")
        p_hi, p_lo = sem("p_hi"), sem("p_lo")
        pv_ready, den_ready, o_ready = sem("pv_ready"), sem("den_ready"), sem("o_ready")
        lg_shift, lg_exp, comb_ready = sem("lg_shift"), sem("lg_exp"), sem("comb_ready")
        gate_step, sum_step = sem("gate_step"), sem("sum_step")
        y_out = sem("y_out")
        block = ctx.enter_context(nc.Block())

        def max_count(b, h, t):
            return b * (HEADS * TT) + (h * TT + t + 1)

        def st_unit(b, h, t):
            last = isinstance(b, int) and (b, h) == (BATCHES - 1, HEADS - 1)
            return h * (TT + 1) + (t if t < ROW_UNIT or last else t + 1)

        def st_count(b, h, t):
            return b * (HEADS * (TT + 1)) + (st_unit(b, h, t) + 2)

        def st_bank(b, h, t):
            return ST[(st_unit(b, h, t) + 1) % 2]

        def row_unit(h):
            return (h - 1) * (TT + 1) + ROW_UNIT

        def row_count(b, h):
            if h == 0 and isinstance(b, int) and b == 0:
                return 1
            return b * (HEADS * (TT + 1)) + (row_unit(h) + 2)

        def row_bank(h):
            return ST[(row_unit(h) + 1) % 2]

        def half_count(b, h, j):
            return b * (HEADS * 2) + (h * 2 + j + 1)

        def head_count(b, h):
            return b * HEADS + (h + 1)

        def dup_count(b, p):
            return 16 * (b * (PAIRS // 2) + (p // 2 + 1))

        late = [(wo[512 * k:512 * (k + 1), :].rearrange("(c p) n -> p c n", p=P),
                 wo_s[:, 0, 4 * k:4 * k + 4, :], wo_s[:, 1, 4 * k:4 * k + 4, :]) for k in range(2)]
        late += [(expert_t[P * c:P * (c + 1), 1024 * k:1024 * (k + 1)],
                  ex_s[:, 0, c, 1024 * k:1024 * (k + 1)], ex_s[:, 1, c, 1024 * k:1024 * (k + 1)])
                 for c in range(LC) for k in range(2)]

        def late_raw(n):
            return late_stage.rearrange("p (c n) -> p c n", c=4) if n < 2 else late_stage

        CONST_POOL = EXPERTS + 5
        CONST_DVE = 4

        def run(engine, step=None, slot=None, before=None, after=None):
            def turn(it):
                if before:
                    before(it)
                for h in range(HEADS):
                    if step:
                        step(it, h)
                    for t in range(TT if slot else 0):
                        slot(it, h, t)
                if after:
                    after(it)
            turn(Iteration(FIRST, 0))
            with engine.Fori(1, BATCHES - 1) as b:
                turn(Iteration(LOOP, b))
            turn(Iteration(LAST, BATCHES - 1))

        @block.sync
        def _(sp):
            sp.dma_start(xin[:, :, :], x_v[:, 0:TT, :]).then_inc(x_in, 16)
            sp.dma_start(kvin[:, :], kv_v[:, 0, :]).then_inc(kv_in, 16)
            sp.dma_start(stage_q.rearrange("p (c n) -> p c n", c=LC),
                         wq.rearrange("(c p) n -> p c n", p=P)).then_inc(wq_in, 16)
            sp.dma_start(stage_k, wk).then_inc(wk_in, 16)
            sp.dma_start(stage_v, wv).then_inc(wv_in, 16)
            sp.dma_start(gates[:, 0:1], g_xattn.partition_broadcast(P)).then_inc(small_in, 16)
            sp.dma_start(gates[:, 1:2], g_ffn.partition_broadcast(P)).then_inc(small_in, 16)
            sp.dma_start(bo_t[:, :], bo.partition_broadcast(P)).then_inc(small_in, 16)
            sp.dma_start(eb[:, :], expert_b).then_inc(small_in, 16)
            sp.dma_start(gt_f[:, :, :], gate_t.rearrange("(c p) e -> p c e", p=P)).then_inc(small_in, 16)

            def copy(it, name):
                kind, p = name
                heads = slice(2 * (p % 2), 2 * (p % 2) + 2)
                dst, src, copied = ((QB[0:HEAD, heads, :], QA[0:HEAD, heads, :], q_dup) if kind == "q" else
                                    (KA[HEAD:P, heads, :], KA[0:HEAD, heads, :], k_dup))
                sp.wait_ge(job_hi, it.done(HI, name))
                sp.dma_start(dst.bitcast(F32), src.bitcast(F32)).then_inc(copied[p % 2], 16)

            for name in [name for name in JOBS[PRO] if name[0] in "qk"]:
                copy(Iteration(PRO, 0), name)

            def before(it):
                if it.kind != LAST:
                    sp.wait_ge(kmax_step, it.b + 1)
                    sp.wait_ge(kv_hi, it.b + 1)
                    sp.wait_ge(kv_lo, it.b + 1)
                    sp.dma_start(kvin[:, :], kv_v[:, bass.ds(it.b + 1, 1), :].rearrange("c a k -> c (a k)"))\
                      .then_inc(kv_in, 16)

            def step(it, h):
                if it.kind == FIRST and h < len(late):
                    if h:
                        sp.wait_ge(late_lo, h)
                    sp.dma_start(late_raw(h), late[h][0]).then_inc(late_in, 16)
                for t in range(TT):
                    for name in jobs_of(it.kind, h, t):
                        if name[0] in "qk":
                            copy(it, name)
                if h == 5 and it.kind != LAST:
                    sp.wait_ge(ln1_done, it.b + 1)
                    sp.wait_ge(x_bias, it.b + 1)
                    sp.dma_start(xin[:, :, :], x_v[:, bass.ds(it.b * TT + TT, TT), :]).then_inc(x_in, 16)

            def after(it):
                if it.kind != FIRST:
                    store(it)

            def store(it):
                m = it.b - 1
                sp.wait_ge(job_free, it.done(JOBS, SUMMED[-1]) + BANKS)
                sp.dma_start(out_v[:, bass.ds(m * TT, TT), :], acc[:, :, :]).then_inc(y_out, 16)

            run(sp, step, before=before, after=after)
            store(Iteration(EPI, BATCHES))
            sp.wait_ge(y_out, 16 * BATCHES + 16)

        @block.gpsimd
        def _(pool):
            pool.memset(ident[:, :], 0.0).then_inc(const_pool, 1)
            for e in range(EXPERTS):
                pool.memset(order[:, e:e + 1], float(EXPERTS - e)).then_inc(const_pool, 1)
            pool.memset(minus_half[:, :], -0.5).then_inc(const_pool, 1)
            pool.memset(v_s[:, 0, :, :, HEAD:HEAD + 1], 1.0).then_inc(const_pool, 1)
            pool.memset(v_s[:, 1, :, :, HEAD:HEAD + 1], 0.0).then_inc(const_pool, 1)
            pool.wait_ge(const_pool, EXPERTS + 4)
            pool.affine_select(out=ident[:, :], in_=ident[:, :], compare_op=ALU.not_equal, fill=1.0, base=0,
                               pattern=[[-1, P]], channel_multiplier=1).then_inc(const_pool, 1)

            def power(n, var, rstd_done):
                pool.wait_ge(var, n)
                pool.tensor_tensor(rstd[:, :], ve[:, :], minus_half[:, :], ALU.pow).then_inc(rstd_done, 1)

            power(1, ln1_var, ln1_rstd)

            def step(it, h):
                for j in range(2):
                    pool.wait_ge(p_hi, max_count(it.b, h, 2 * j + 1))
                    pool.tensor_tensor(p_s[:, h % 2, 1, 2 * j:2 * j + 2, :], pf[:, 2 * j:2 * j + 2, :],
                                       p_s[:, h % 2, 0, 2 * j:2 * j + 2, :], ALU.subtract).then_inc(p_lo, 1)
                    if (h, j) == (3, 0) and it.kind != FIRST:
                        power(it.b, ln2_var, ln2_rstd)
                if it.kind == FIRST and h < len(late):
                    pool.wait_ge(late_hi, h + 1)
                    pool.tensor_tensor(late[h][2], late_raw(h), late[h][1].bitcast(F32), ALU.subtract)\
                        .then_inc(late_lo, 1)
                if h == 3:
                    pool.wait_ge(x_in, 16 * it.b + 16)
                    if it.kind == FIRST:
                        pool.wait_ge(const_dve, CONST_DVE)
                    else:
                        pool.wait_ge(job_free, it.done(JOBS, ("wo", ROUNDS - 1, MT - 1)) + BANKS)
                    pool.tensor_tensor(x2[:, :, :], xin[:, :, :],
                                       bo_t[:, :].unsqueeze(1).broadcast_to([P, TT, DIM]), ALU.add)\
                        .then_inc(x_bias, 1)
                if h == 10 and it.kind != LAST:
                    power(it.b + 2, ln1_var, ln1_rstd)

            run(pool, step)
            power(BATCHES, ln2_var, ln2_rstd)

        @block.scalar
        def _(act):
            act.wait_ge(kv_in, 16)
            act.activation(kv_s[:, 0, :], kvin[:, :], ACT.Copy).then_inc(kv_hi, 1)
            act.wait_ge(wq_in, 16)
            act.activation(wq_s[:, 0, :, :], stage_q.rearrange("p (c n) -> p c n", c=LC), ACT.Copy).then_inc(w_hi, 1)
            act.wait_ge(wk_in, 16)
            act.activation(wk_s[:, 0, :], stage_k, ACT.Copy).then_inc(w_hi, 1)
            act.wait_ge(wv_in, 16)
            act.activation(wv_s[:, 0, :], stage_v, ACT.Copy).then_inc(w_hi, 1)
            act.wait_ge(small_in, 5 * 16)
            act.activation(gt_s[:, 0, :, :], gt_f[:, :, :], ACT.Copy).then_inc(w_hi, 1)
            act.activation(tg[:, :], gates[:, :], ACT.Tanh).then_inc(tanh_done, 1)

            def take_hi(it, name):
                act.wait_ge(job_ready, it.done(JOBS, name))
                m = MB[it.bank(name)]
                kind = name[0]
                if kind in ("q", "k"):
                    dst, s = (QA if kind == "q" else KA), 2 * (name[1] % 2)
                    act.activation(dst[0:HEAD, s, :], m[0:HEAD, :], ACT.Copy)
                    last = act.activation(dst[0:HEAD, s + 1, :], m[HEAD:P, :], ACT.Copy)
                elif kind == "xt":
                    last = act.activation(xt_s[:, 0, name[1], :], m[:, :], ACT.Copy)
                elif kind == "x2t":
                    last = act.activation(x2t_s[:, 0, name[1], :], m[:, :], ACT.Copy)
                elif kind == "ot":
                    last = act.activation(ot_s[:, 0, name[1] % GROUP, :], m[:, :], ACT.Copy)
                else:
                    _, t, g = name
                    act.wait_ge(scale_done, it.b + 1 if g or it.kind == PRO else it.b + 2)
                    last = act.activation(v_s[:, 0, t, g * HH:(g + 1) * HH, 0:HEAD],
                                          m[:, :].rearrange("p (h d) -> p h d", d=HEAD), ACT.Copy,
                                          scale=v_mul[:, 0:1])
                last.then_inc(job_hi, 1)

            def take_row(b, h):
                act.wait_ge(st_ready, row_count(b, h))
                act.activation(QB[HEAD:HEAD + 1, h % 4, :], row_bank(h)[HEAD:HEAD + 1, :], ACT.Copy)\
                   .then_inc(st_free, 1)

            pro = Iteration(PRO, 0)
            for name in HI[PRO]:
                take_hi(pro, name)
            take_row(0, 0)

            def slot(it, h, t):
                b, kind = it.b, it.kind
                if (h, t) == (HEADS - 3, 0) and kind != LAST:
                    act.wait_ge(kv_in, 16 * b + 32)
                    act.wait_ge(job_ready, it.done(JOBS, ("k", PAIRS - 1)))
                    act.activation(kv_s[:, 0, :], kvin[:, :], ACT.Copy).then_inc(kv_hi, 1)
                for name in taken_in(kind, h, t):
                    if name[0] in SPLIT:
                        take_hi(it, name)
                if t == ROW_UNIT and (h + 1 < HEADS or kind != LAST):
                    take_row(b, h + 1)
                act.wait_ge(st_ready, st_count(b, h, t))
                if t % 2 == 0:
                    act.wait_ge(p_lo, half_count(b, h - 1, t // 2) + 2)
                act.activation(pf[:, t, :], st_bank(b, h, t)[:, :], ACT.Exp, bias=P_SHIFT, scale=SCALE)\
                   .then_inc(st_free, 1)
                if t:
                    probabilities(b, h, t - 1)
                elif h or kind != FIRST:
                    probabilities(b, h - 1, TT - 1)
                if kind != FIRST and (h, t) == LOGITS_AT:
                    logit_exp(b - 1)
                if kind == FIRST and t == TT - 1 and h < len(late):
                    act.wait_ge(late_in, 16 * (h + 1))
                    act.activation(late[h][1], late_raw(h), ACT.Copy).then_inc(late_hi, 1)

            def probabilities(b, h, t):
                act.wait_ge(st_free, st_count(b, h, t) + 2)
                if t == 0:
                    act.wait_ge(pv_ready, head_count(b, h - 2) + 2)
                act.activation(p_s[:, h % 2, 0, t, :], pf[:, t, :], ACT.Copy).then_inc(p_hi, 1)

            def logit_exp(m):
                act.wait_ge(lg_shift, m + 1)
                act.activation(prob[:, :, :], logit[:, :, :], ACT.Exp).then_inc(lg_exp, 1)

            run(act, slot=slot)
            probabilities(BATCHES - 1, HEADS - 1, TT - 1)
            for name in HI[EPI]:
                take_hi(Iteration(EPI, BATCHES), name)
            logit_exp(BATCHES - 1)

        @block.vector
        def _(dve):
            dve.memset(ones[:, :], 1.0).then_inc(job_free, BANKS)
            dve.memset(rden[:, :], 0.0).then_inc(max_free, 2)
            dve.memset(r1[:, :], 0.0).then_inc(st_free, 2)
            dve.memset(r2[:, :], 0.0).then_inc(p_lo, 2)
            dve.memset(ve[:, :], 0.0).then_inc(pv_ready, 2)
            dve.memset(rstd[:, :], 0.0).then_inc(o_ready, 1)
            dve.memset(p2[:, :, :], 0.0).then_inc(y_out, 16)
            dve.memset(KB[HEAD:HEAD + 1, :, :].bitcast(F32), 1.0).then_inc(const_dve, 1)

            def statistics(src, n, count, var):
                for t in range(TT):
                    last = dve.bn_stats(stats[:, t, :], src[:, t, :])
                last.then_inc(n, 1)
                dve.wait_ge(n, count)
                dve.memset(ve[:, :], 0.0)
                for t in range(TT):
                    last = dve.bn_aggr(mv[:, t, :], stats[:, t, :])
                last.then_inc(n, 1)
                dve.wait_ge(n, count + 1)
                dve.tensor_scalar(ve[:, :], mv[:, :, 1], EPS, None, ALU.add).then_inc(var, 1)

            def apply(src, rstd_done, count, done):
                dve.wait_ge(rstd_done, count)
                for t in range(TT):
                    last = dve.tensor_scalar(xn[:, t, :], src[:, t, :], mv[:, t, 0:1], rstd[:, t:t + 1],
                                             ALU.subtract, ALU.mult)
                last.then_inc(done, 1)

            def bound(b):
                dve.wait_ge(kv_in, 16 * b + 16)
                dve.tensor_reduce(kmax[:, 0:1], kvin[:, :], AX.X, ALU.max, apply_absolute_value=True)\
                   .then_inc(kmax_step, 1)
                dve.wait_ge(kmax_step, b + 1)
                dve.tensor_tensor(kmax[:, 1:2], kmax[:, 0:1], wv_max[:, :], ALU.mult).then_inc(kmax_done, 1)

            def context_lo(b):
                dve.wait_ge(kv_hi, b + 1)
                dve.tensor_tensor(kv_s[:, 1, :], kvin[:, :], kv_s[:, 0, :].bitcast(F32), ALU.subtract)\
                   .then_inc(kv_lo, 1)

            def take(it, name):
                m = MB[it.bank(name)]
                kind = name[0]
                if kind not in SPLIT:
                    dve.wait_ge(job_ready, it.done(JOBS, name))
                if kind == "wo":
                    _, r, j = name
                    if r == 0 and j == 0:
                        dve.wait_ge(x_bias, it.b + 1)
                    if r == ROUNDS - 1 and j == 0:
                        dve.wait_ge(late_lo, len(late))
                        dve.wait_ge(y_out, 16 * it.b)
                    dst = acc if r == ROUNDS - 1 else x2
                    last = dve.scalar_tensor_tensor(dst[:, 2 * j:2 * j + 2, :], m[:, :].rearrange("p (a n) -> p a n", a=2),
                                                    tg[:, 0:1], x2[:, 2 * j:2 * j + 2, :], ALU.mult, ALU.add)
                elif kind == "bound":
                    last = dve.tensor_scalar(v_div[:, :], m[:, 0:1], 1.0 / V_RANGE, 1e-30, ALU.mult, ALU.max)
                elif kind in ("router", "gates"):
                    last = dve.tensor_copy(comb_t, m[0:EXPERTS, :])
                elif kind == "logits":
                    last = dve.tensor_copy(m1[:, :, :], m[:, 0:TT * EXPERTS].rearrange("p (t e) -> p t e", t=TT))
                elif kind == "bias":
                    j = name[1]
                    dve.wait_ge(job_free, it.done(JOBS, SUMMED[SUMMED.index(name) - 1]) + BANKS)
                    last = dve.tensor_tensor(acc[:, 2 * j:2 * j + 2, :], m[:, :].rearrange("p (a n) -> p a n", a=2),
                                             acc[:, 2 * j:2 * j + 2, :], ALU.add)
                elif kind == "expert":
                    _, t, e = name
                    if (t, e) == (0, 0):
                        dve.wait_ge(comb_ready, it.b)
                    else:
                        dve.wait_ge(job_free, it.done(JOBS, SUMMED[SUMMED.index(name) - 1]) + BANKS)
                    for i in range(2):
                        last = dve.scalar_tensor_tensor(acc[:, t, :], m[:, DIM * i:DIM * (i + 1)],
                                                        comb[:, t, 2 * e + i:2 * e + i + 1], acc[:, t, :],
                                                        ALU.mult, ALU.add)
                        if i == 0:
                            last.then_inc(sum_step, 1)
                            dve.wait_ge(sum_step, (it.b - 1) * (TT * EC) + (t * EC + e + 1))
                if kind not in SPLIT:
                    last.then_inc(job_free, 1)
                    if kind == "bound":
                        dve.wait_ge(job_free, it.done(JOBS, name) + BANKS)
                        dve.reciprocal(v_mul[:, :], v_div[:, :]).then_inc(scale_done, 1)
                        dve.wait_ge(scale_done, 1 if it.kind == PRO else it.b + 2)
                    return
                dve.wait_ge(job_hi, it.done(HI, name))
                if kind == "q":
                    s = 2 * (name[1] % 2)
                    for i in range(2):
                        last = dve.tensor_tensor(QA[HEAD:P, s + i, :], m[HEAD * i:HEAD * i + HEAD, :],
                                                 QA[0:HEAD, s + i, :].bitcast(F32), ALU.subtract)
                elif kind == "k":
                    s = 2 * (name[1] % 2)
                    for i in range(2):
                        last = dve.tensor_tensor(KB[0:HEAD, s + i, :], m[HEAD * i:HEAD * i + HEAD, :],
                                                 KA[0:HEAD, s + i, :].bitcast(F32), ALU.subtract)
                elif kind == "xt":
                    last = dve.tensor_tensor(xt_s[:, 1, name[1], :], m[:, :], xt_s[:, 0, name[1], :].bitcast(F32),
                                             ALU.subtract)
                elif kind == "x2t":
                    last = dve.tensor_tensor(x2t_s[:, 1, name[1], :], m[:, :], x2t_s[:, 0, name[1], :].bitcast(F32),
                                             ALU.subtract)
                elif kind == "ot":
                    s = name[1] % GROUP
                    last = dve.tensor_tensor(ot_s[:, 1, s, :], m[:, :], ot_s[:, 0, s, :].bitcast(F32), ALU.subtract)
                else:
                    _, t, g = name
                    last = dve.scalar_tensor_tensor(v_s[:, 1, t, g * HH:(g + 1) * HH, 0:HEAD],
                                                    m[:, :].rearrange("p (h d) -> p h d", d=HEAD), v_mul[:, 0:1],
                                                    v_s[:, 0, t, g * HH:(g + 1) * HH, 0:HEAD],
                                                    ALU.mult, ALU.subtract)
                last.then_inc(job_free, 1)

            def maximum(b, h, t):
                dve.wait_ge(max_ready, max_count(b, h, t))
                dve.tensor_reduce(nmax[:, h % 2, t:t + 1], MX[t % 2][:, :], AX.X, ALU.max, negate=True)\
                   .then_inc(max_free, 1)

            def normalise(b, h):
                heads = PV[:, 0:TT * (HEAD + 1)].rearrange("p (t d) -> p t d", t=TT)
                dve.wait_ge(pv_ready, head_count(b, h) + 2)
                dve.reciprocal(rden[:, :], heads[:, :, HEAD]).then_inc(den_ready, 1)
                dve.wait_ge(den_ready, head_count(b, h))
                side, col = h % HEADS // 2 % 2, HEAD * (h % 2)
                dve.scalar_tensor_tensor(o_n[:, side, :, col:col + HEAD], heads[:, :, 0:HEAD], o_mul[:, 0:1],
                                         rden[:, :].unsqueeze(2).broadcast_to([P, TT, HEAD]),
                                         ALU.mult, ALU.mult).then_inc(o_ready, 1)

            dve.wait_ge(x_in, 16)
            statistics(xin, ln1_step, 1, ln1_var)
            context_lo(0)
            apply(xin, ln1_rstd, 1, ln1_done)
            dve.wait_ge(w_hi, 1)
            dve.tensor_tensor(wq_s[:, 1, :, :], stage_q.rearrange("p (c n) -> p c n", c=LC),
                              wq_s[:, 0, :, :].bitcast(F32), ALU.subtract).then_inc(w_lo, 1)
            dve.wait_ge(w_hi, 2)
            dve.tensor_tensor(wk_s[:, 1, :], stage_k, wk_s[:, 0, :].bitcast(F32), ALU.subtract).then_inc(w_lo, 1)
            dve.wait_ge(w_hi, 3)
            dve.tensor_tensor(wv_s[:, 1, :], stage_v, wv_s[:, 0, :].bitcast(F32), ALU.subtract).then_inc(w_lo, 1)
            dve.tensor_reduce(wv_max[:, :], stage_v, AX.X, ALU.max, apply_absolute_value=True).then_inc(const_dve, 1)
            dve.wait_ge(const_dve, 2)
            bound(0)
            dve.wait_ge(w_hi, 4)
            dve.tensor_tensor(gt_s[:, 1, :, :], gt_f[:, :, :], gt_s[:, 0, :, :].bitcast(F32), ALU.subtract)\
               .then_inc(w_lo, 1)
            dve.wait_ge(const_pool, EXPERTS + 5)
            dve.tensor_copy(ident_r[:, :], ident[:, :]).then_inc(const_dve, 1)
            dve.wait_ge(tanh_done, 1)
            dve.tensor_scalar(bo_t[:, :], bo_t[:, :], tg[:, 0:1], None, ALU.mult).then_inc(const_dve, 1)
            pro = Iteration(PRO, 0)
            for n, name in enumerate(JOBS[PRO]):
                take(pro, name)
                if name == ("k", 0):
                    for t in range(TT):
                        maximum(0, 0, t)
            for t in range(TT // 2):
                maximum(0, 1, t)

            def outputs_scale(b):
                dve.wait_ge(scale_done, b + 1)
                dve.tensor_copy(o_mul[:, :], v_div[:, :]).then_inc(o_mul_done, 1)
                dve.wait_ge(o_mul_done, b + 1)

            def slot(it, h, t):
                b, kind = it.b, it.kind
                taken = taken_in(kind, h, t)
                first_split = min([n for n, name in enumerate(taken) if name[0] in SPLIT], default=len(taken))
                if t == 1 and (h >= 2 or kind != FIRST):
                    if h == 2:
                        outputs_scale(b)
                    normalise(b, h - 2)
                for name in taken[:first_split]:
                    take(it, name)
                if maximum_at(kind, h, t):
                    maximum(b, *maximum_at(kind, h, t))
                for name in taken[first_split:]:
                    take(it, name)
                if ("logits",) in taken:
                    route(it, 0)
                if kind != FIRST:
                    if (h, t) in ROUTE_SLOTS:
                        route(it, 1 + ROUTE_SLOTS.index((h, t)))
                    if (h, t) == (3, 0):
                        dve.wait_ge(job_free, it.done(JOBS, ("wo", ROUNDS - 1, MT - 1)) + BANKS)
                        second_norm(b - 1)
                    if (h, t) == (3, 3):
                        apply(acc, ln2_rstd, b, ln2_done)
                if kind != LAST:
                    if (h, t) == (8, 3):
                        bound(b + 1)
                    if (h, t) == (10, 1):
                        dve.wait_ge(x_in, 16 * b + 32)
                        statistics(xin, ln1_step, 2 * b + 3, ln1_var)
                    if (h, t) == (11, 2):
                        apply(xin, ln1_rstd, b + 2, ln1_done)
                    if (h, t) == (HEADS - 3, 1):
                        context_lo(b + 1)

            def second_norm(m):
                statistics(acc, ln2_step, 2 * m + 1, ln2_var)

            GATE_STEPS = 17

            def over(v):
                return v[:, :].unsqueeze(2).broadcast_to([P, TT, EXPERTS])

            def route(it, part):
                m = it.b - 1
                n = [(0, 1, 4, 7, 10, 13, 16)[part]]

                def then(ins):
                    n[0] += 1
                    ins.then_inc(gate_step, 1)
                    dve.wait_ge(gate_step, m * GATE_STEPS + n[0])

                def candidates(src):
                    then(dve.tensor_reduce(r1[:, :], src[:, :, :], AX.X, ALU.max))
                    then(dve.tensor_tensor(w1[:, :, :], src[:, :, :], over(r1), ALU.is_equal))
                    then(dve.tensor_tensor(w1[:, :, :], w1[:, :, :],
                                           order[:, :].unsqueeze(1).broadcast_to([P, TT, EXPERTS]), ALU.mult))

                def first(mask):
                    then(dve.tensor_reduce(r1[:, :], w1[:, :, :], AX.X, ALU.max))
                    then(dve.tensor_tensor(mask[:, :, :], w1[:, :, :], over(r1), ALU.is_equal))

                if part == 0:
                    dve.wait_ge(job_free, it.done(JOBS, ("logits",)) + BANKS)
                    then(dve.tensor_reduce(r1[:, :], m1[:, :, :], AX.X, ALU.max, negate=True))
                    dve.tensor_tensor(logit[:, :, :], m1[:, :, :], over(r1), ALU.add).then_inc(lg_shift, 1)
                elif part == 1:
                    dve.wait_ge(lg_exp, m + 1)
                    then(dve.tensor_reduce(r1[:, :], prob[:, :, :], AX.X, ALU.add))
                    then(dve.reciprocal(r2[:, :], r1[:, :]))
                    then(dve.tensor_tensor(prob[:, :, :], prob[:, :, :], over(r2), ALU.mult))
                elif part == 2:
                    candidates(prob)
                elif part == 3:
                    first(m1)
                    then(dve.scalar_tensor_tensor(p2[:, :, :], m1[:, :, :], -2.0, prob[:, :, :], ALU.mult, ALU.add))
                elif part == 4:
                    candidates(p2)
                elif part == 5:
                    first(m2)
                    then(dve.tensor_tensor(m2[:, :, :], m1[:, :, :], m2[:, :, :], ALU.add))
                else:
                    then(dve.tensor_tensor(m2[:, :, :], prob[:, :, :], m2[:, :, :], ALU.mult))
                    assert n[0] == GATE_STEPS
                    dve.tensor_scalar(comb[:, :, :], m2[:, :, :], tg[:, 1:2], None, ALU.mult).then_inc(comb_ready, 1)

            run(dve, slot=slot)
            epi = Iteration(EPI, BATCHES)
            normalise(BATCHES - 1, HEADS - 2)
            normalise(BATCHES - 1, HEADS - 1)
            for name in JOBS[EPI]:
                take(epi, name)
                if name == ("wo", ROUNDS - 1, MT - 1):
                    dve.wait_ge(job_free, epi.done(JOBS, name) + BANKS)
                    second_norm(BATCHES - 1)
                    apply(acc, ln2_rstd, BATCHES, ln2_done)
                if name == ("logits",):
                    for part in range(1 + len(ROUTE_SLOTS)):
                        route(epi, part)

        @block.tensor
        def _(pe):
            def parts(dst, terms):
                n = 3 * len(terms)
                k = 0
                for (s_hi, s_lo), (m_hi, m_lo) in terms:
                    for s, m in ((s_hi, m_hi), (s_hi, m_lo), (s_lo, m_hi)):
                        last = pe.matmul(dst, s, m, start=(k == 0), stop=(k == n - 1))
                        k += 1
                return last

            def tile(t):
                return slice(t * P, (t + 1) * P)

            def turned(bank_, src):
                for t in range(TT):
                    last = pe.transpose(bank_[:, tile(t)], src(t), ident[:, :])
                return last

            def produce(it, name):
                kind = name[0]
                m = MB[it.bank(name)]
                n = it.done(JOBS, name)
                if kind == "xt":
                    pe.wait_ge(ln1_done, it.b + 1 if it.kind == PRO else it.b + 2)
                elif kind == "ot":
                    p = name[1]
                    if p == PAIRS - 1:
                        pe.wait_ge(o_ready, head_count(it.b, -1) + 1)
                    else:
                        pe.wait_ge(o_ready, head_count(it.b, 2 * p + 1) + 1)
                elif kind == "wo":
                    pe.wait_ge(job_free, it.done(JOBS, ("ot", name[1] * GROUP + GROUP - 1)) + BANKS)
                    if it.kind == FIRST:
                        pe.wait_ge(late_lo, 2)
                elif kind == "k" and it.kind != PRO and name[1] == 0:
                    pe.wait_ge(kv_lo, it.b + 2)
                elif kind == "bound":
                    pe.wait_ge(kmax_done, 1 if it.kind == PRO else it.b + 2)
                elif kind == "x2t":
                    pe.wait_ge(ln2_done, it.b)
                elif kind in ("router", "logits"):
                    before = {"router": ("x2t", LC - 1), "logits": ("router",)}[kind]
                    pe.wait_ge(job_free, it.done(JOBS, before) + BANKS)
                elif kind == "gates":
                    pe.wait_ge(comb_ready, it.b)
                elif kind == "bias" and name[1] == 0:
                    pe.wait_ge(job_free, it.done(JOBS, ("gates",)) + BANKS)
                elif kind == "q" and it.kind != PRO and name[1] == 0:
                    pe.wait_ge(job_free, it.done(JOBS, ("xt", LC - 1)) + BANKS)
                pe.wait_ge(job_free, n)
                if kind == "xt":
                    c = name[1]
                    last = turned(m, lambda t: xn[:, t, c * P:(c + 1) * P])
                elif kind == "q":
                    cols = slice(name[1] * P, (name[1] + 1) * P)
                    last = parts(m[:, :], [((wq_s[:, 0, c, cols], wq_s[:, 1, c, cols]),
                                            (xt_s[:, 0, c, :], xt_s[:, 1, c, :])) for c in range(LC)])
                elif kind == "k":
                    cols = slice(name[1] * P, (name[1] + 1) * P)
                    last = parts(m[:, :], [((wk_s[:, 0, cols], wk_s[:, 1, cols]), (kv_s[:, 0, :], kv_s[:, 1, :]))])
                elif kind == "v":
                    _, t, g = name
                    cols = slice(g * 512, (g + 1) * 512)
                    last = parts(m[:, :], [((kv_s[:, 0, tile(t)], kv_s[:, 1, tile(t)]),
                                            (wv_s[:, 0, cols], wv_s[:, 1, cols]))])
                elif kind == "bound":
                    last = pe.matmul(m[:, 0:1], kmax[:, 1:2].broadcast_to([P, P]), ones[:, :], start=True, stop=True)
                elif kind == "x2t":
                    last = turned(m, lambda t: xn[:, t, name[1] * P:(name[1] + 1) * P])
                elif kind == "router":
                    last = parts(m[0:EXPERTS, :], [((gt_s[:, 0, c, :], gt_s[:, 1, c, :]),
                                                    (x2t_s[:, 0, c, :], x2t_s[:, 1, c, :])) for c in range(LC)])
                elif kind == "logits":
                    for t in range(TT):
                        last = pe.matmul(m[:, t * EXPERTS:(t + 1) * EXPERTS], comb_t[:, tile(t)],
                                         ident[0:EXPERTS, 0:EXPERTS], start=True, stop=True)
                elif kind == "gates":
                    for t in range(TT):
                        last = pe.transpose(m[0:EXPERTS, tile(t)], comb[:, t, :], ident[:, :])
                elif kind == "bias":
                    for i in range(2):
                        last = pe.matmul(m[:, DIM * i:DIM * (i + 1)], comb_t[:, tile(2 * name[1] + i)],
                                         eb[:, :], start=True, stop=True)
                elif kind == "expert":
                    _, t, e = name
                    cols = slice(e * 512, (e + 1) * 512)
                    last = parts(m[:, :], [((x2t_s[:, 0, c, tile(t)], x2t_s[:, 1, c, tile(t)]),
                                            (ex_s[:, 0, c, cols], ex_s[:, 1, c, cols])) for c in range(LC)])
                elif kind == "ot":
                    last = turned(m, lambda t: o_n[:, name[1] % 2, t, :])
                else:
                    _, r, j = name
                    for i in range(2):
                        q = tile(2 * j + i)
                        last = parts(m[:, DIM * i:DIM * (i + 1)],
                                     [((ot_s[:, 0, k, q], ot_s[:, 1, k, q]),
                                       (wo_s[:, 0, r * GROUP + k, :], wo_s[:, 1, r * GROUP + k, :]))
                                      for k in range(GROUP)])
                last.then_inc(job_ready, 1)

            def maximum(b, h, t):
                s = h % 4
                pe.wait_ge(max_free, max_count(b, h, t))
                pe.matmul(MX[t % 2][:, :], QA[0:HEAD, s, tile(t)], KA[0:HEAD, s, :], start=True, stop=True)\
                  .then_inc(max_ready, 1)

            def row(b, h):
                pe.wait_ge(max_free, max_count(b, h, TT - 1) + 2)
                pe.wait_ge(st_free, row_count(b, h))
                for t in range(TT):
                    last = pe.matmul(row_bank(h)[:, tile(t)], nmax[:, h % 2, t:t + 1].broadcast_to([P, P]),
                                     ident_r[:, :], start=True, stop=True)
                last.then_inc(st_ready, 1)

            def scores(b, h, t):
                s = h % 4
                pe.wait_ge(st_free, st_count(b, h, t))
                pe.matmul(st_bank(b, h, t)[:, :], KA[:, s, tile(t)], QA[:, s, :], start=True, stop=False)
                pe.matmul(st_bank(b, h, t)[:, :], KB[0:HEAD + 1, s, tile(t)], QB[0:HEAD + 1, s, :],
                          start=False, stop=True).then_inc(st_ready, 1)

            def values(b, h, half):
                if half == 0:
                    pe.wait_ge(p_lo, half_count(b, h, 1) + 2)
                    pe.wait_ge(o_ready, head_count(b, h))
                for t in range(half * TT // 2, (half + 1) * TT // 2):
                    for k in range(TT):
                        for n, (i, j) in enumerate(((0, 0), (0, 1), (1, 0))):
                            last = pe.matmul(PV[:, t * (HEAD + 1):(t + 1) * (HEAD + 1)],
                                             p_s[:, h % 2, i, k, tile(t)], v_s[:, j, k, h % HEADS, :],
                                             start=(k == 0 and n == 0), stop=(k == TT - 1 and n == 2))
                if half:
                    last.then_inc(pv_ready, 1)

            pe.wait_ge(const_pool, EXPERTS + 5)
            pro = Iteration(PRO, 0)
            for name in JOBS[PRO]:
                if name == ("q", 0):
                    pe.wait_ge(w_lo, 2)
                    pe.wait_ge(job_free, pro.done(JOBS, ("xt", LC - 1)) + BANKS)
                    pe.wait_ge(kv_lo, 1)
                if name == ("v", 0, 0):
                    pe.wait_ge(w_lo, 3)
                    pe.wait_ge(job_hi, pro.done(HI, ("k", 0)))
                    for t in range(TT):
                        maximum(0, 0, t)
                produce(pro, name)
            pe.wait_ge(job_hi, pro.done(HI, ("k", 0)))
            for t in range(TT // 2):
                maximum(0, 1, t)
            pe.wait_ge(const_dve, 3)
            row(0, 0)

            def slot(it, h, t):
                b, kind = it.b, it.kind
                p, ahead = h // 2, (h + 2) // 2 % PAIRS
                if h % 2 == 0 and t == 0:
                    pe.wait_ge(job_free, (it.done if p else it.done_before)(JOBS, ("k", p)) + BANKS)
                    pe.wait_ge(q_dup[p % 2], dup_count(b, p))
                    pe.wait_ge(k_dup[p % 2], dup_count(b, p))
                if h % 2 == 0 and t == TT // 2 and maximum_at(kind, h, t):
                    pe.wait_ge(job_hi, it.done(HI, ("k", ahead)))
                if t == 0:
                    pe.wait_ge(st_free, row_count(b, h) + 2)
                scores(b, h, t)
                if maximum_at(kind, h, t):
                    maximum(b, *maximum_at(kind, h, t))
                if t in VALUES_SLOTS:
                    back, half = VALUES_SLOTS[t]
                    if h >= back or kind != FIRST:
                        values(b, h - back, half)
                for name in jobs_of(kind, h, t):
                    produce(it, name)
                if t == ROW_UNIT - 1 and (h + 1 < HEADS or kind != LAST):
                    row(b, h + 1)

            run(pe, slot=slot)
            epi = Iteration(EPI, BATCHES)
            values(BATCHES - 1, HEADS - 2, 1)
            values(BATCHES - 1, HEADS - 1, 0)
            values(BATCHES - 1, HEADS - 1, 1)
            for name in JOBS[EPI]:
                produce(epi, name)


def kernel(x, ctx_512, g_xattn, g_ffn, L0_xattn_Wq, L0_xattn_Wk, L0_xattn_Wv, L0_xattn_Wo, L0_xattn_bo,
           L0_ffn_gate_w, L0_ffn_expert_w, L0_ffn_expert_b):
    import numpy as np
    import concourse.bacc as bacc
    from concourse.bass_utils import run_bass_kernel_spmd

    nc = bacc.Bacc("TRN2", target_bir_lowering=False, num_devices=1)
    ins = {
        "x": x,
        "kv_t": np.asarray(ctx_512).transpose(0, 2, 1),
        "g_xattn": g_xattn,
        "g_ffn": g_ffn,
        "wq": L0_xattn_Wq, "wk": L0_xattn_Wk, "wv": L0_xattn_Wv, "wo": L0_xattn_Wo, "bo": L0_xattn_bo,
        "gate_t": np.asarray(L0_ffn_gate_w).T,
        "expert_t": np.asarray(L0_ffn_expert_w).transpose(2, 0, 1).reshape(DIM, EXPERTS * DIM),
        "expert_b": L0_ffn_expert_b,
    }
    ins = {n: np.ascontiguousarray(a) for n, a in ins.items()}
    aps = {n: nc.dram_tensor(n, a.shape, mybir.dt.from_np(a.dtype), kind="ExternalInput").ap()
           for n, a in ins.items()}
    out = nc.dram_tensor("out", (BATCHES, TOKENS, DIM), F32, kind="ExternalOutput").ap()
    build(nc, out=out, **aps)
    r = run_bass_kernel_spmd(nc, [ins], core_ids=[0])
    return r.results[0]["out"]
```

```python
import math
from contextlib import ExitStack

import concourse.bass as bass
from concourse import mybir

F32 = mybir.dt.float32
F32R = mybir.dt.float32r
F16 = mybir.dt.float16
ALU = mybir.AluOpType
ACT = mybir.ActivationFunctionType
AX = mybir.AxisListType

P = 128
BATCHES, TOKENS, DIM = 8, 512, 256
CTX, HEADS, HEAD = 128, 16, 64
INNER = HEADS * HEAD
EXPERTS = 8
TT = TOKENS // P
LC = DIM // P
PAIRS = HEADS // 2
HALVES = INNER // 512
EC = EXPERTS * DIM // 512
GROUP = 2
EPS = 1e-5
SCALE = HEAD ** -0.5
P_SHIFT = 7 * math.log(2.0)
V_RANGE = 30000.0

ROUNDS = PAIRS // GROUP
MT = TT // 2
HH = HEADS // HALVES

PRO, FIRST, LOOP, LAST, EPI = "pro", "first", "loop", "last", "epi"


PLACED = {
    (0, 0): [("k", 1)],
    (1, 0): [("v", 0, 1)], (1, 2): [("ot", 7)], (1, 3): [("q", 2)],
    (2, 0): [("k", 2)], (2, 1): [("wo", 3, 0)], (2, 3): [("wo", 3, 1)],
    (3, 1): [("v", 1, 1)], (3, 2): [("ot", 0)], (3, 3): [("q", 3)],
    (4, 0): [("k", 3)], (4, 1): [("v", 2, 1)], (4, 3): [("x2t", 0), ("x2t", 1)],
    (5, 1): [("router",)], (5, 2): [("ot", 1)], (5, 3): [("q", 4)],
    (6, 0): [("k", 4), ("logits",)], (6, 2): [("v", 3, 1)], (6, 3): [("wo", 0, 0), ("wo", 0, 1)],
    (7, 1): [("ot", 2)], (7, 3): [("q", 5)],
    (8, 0): [("k", 5)], (8, 1): [("gates",), ("expert", 0, 0)], (8, 2): [("expert", 0, 1)],
    (8, 3): [("expert", 0, 2)],
    (9, 1): [("expert", 0, 3), ("expert", 1, 0), ("bias", 1), ("bound",)], (9, 2): [("ot", 3)],
    (9, 3): [("q", 6), ("k", 6)],
    (10, 1): [("bias", 0), ("wo", 1, 0)], (10, 3): [("expert", 1, 1), ("expert", 1, 2)],
    (11, 0): [("expert", 1, 3)], (11, 1): [("wo", 1, 1)], (11, 2): [("ot", 4)],
    (11, 3): [("q", 7), ("expert", 2, 0)],
    (12, 0): [("k", 7)], (12, 1): [("xt", 0)], (12, 2): [("expert", 2, 1)], (12, 3): [("expert", 2, 2), ("xt", 1)],
    (13, 1): [("expert", 2, 3)], (13, 2): [("ot", 5)], (13, 3): [("q", 0), ("k", 0)],
    (14, 0): [("wo", 2, 1)], (14, 1): [("expert", 3, 0), ("v", 0, 0)], (14, 2): [("expert", 3, 1), ("wo", 2, 0)],
    (14, 3): [("v", 2, 0)],
    (15, 0): [("v", 1, 0), ("expert", 3, 2)], (15, 1): [("expert", 3, 3)], (15, 2): [("v", 3, 0), ("ot", 6)],
    (15, 3): [("q", 1)],
}
FIRST_VALUES = {(0, 1): [("v", 0, 0, 0)], (0, 2): [("v", 1, 0, 0)], (0, 3): [("v", 2, 0, 0)], (1, 0): [("v", 3, 0, 0)]}

VALUES_SLOT = 0
VALUES_BACK = 2
NORMALISE_SLOT = 1
ROW_UNIT = 3
PE_ORDER = (
    ('scores maximum row values jobs',
     'maximum scores jobs row values',
     'scores maximum values jobs row',
     'maximum scores jobs values row'),
    ('scores maximum row values jobs',
     'maximum scores jobs row values',
     'scores values maximum jobs row',
     'maximum scores jobs values row'))
ACT_ORDER = (
    ('hi exp copy',
     'copy hi exp',
     'hi exp copy',
     'hi exp copy'),
    ('hi copy exp',
     'copy hi exp',
     'hi exp copy',
     'exp hi copy'))
DVE_ORDER = (
    ('normalise whole maximum lo',
     'normalise whole maximum lo',
     'normalise whole maximum lo',
     'lo normalise maximum whole'),
    ('normalise whole maximum lo',
     'normalise whole maximum lo',
     'normalise whole lo maximum',
     'lo normalise maximum whole'))
LN2_AT, LN2_APPLY_AT = (3, 0), (3, 2)
LN2_POWER_AT = (3, 0)
LOGITS_AT = (6, 3)
ROUTE_SLOTS = [(6, 3), (7, 0), (7, 1), (7, 2), (7, 3), (8, 0)]
BOUND_AT = (9, 0)
LN1_AT, LN1_APPLY_AT = (10, 3), (11, 2)
KV_HI_AT, KV_LO_AT = (13, 1), (13, 1)


def jobs_of(kind, h, t):
    jobs = PLACED.get((h, t), []) + (FIRST_VALUES.get((h, t), []) if kind == FIRST else [])
    absent = {FIRST: [("ot", PAIRS - 1)] + [("wo", ROUNDS - 1, j) for j in range(MT)] + EXPERT_JOBS,
              LOOP: [], LAST: NEXT_JOBS}[kind]
    return [name for name in jobs if name not in absent]


NEXT_JOBS = [("xt", 0), ("xt", 1), ("q", 0), ("k", 0), ("q", 1), ("bound",)] + [("v", t, 0) for t in range(TT)]
SUMMED = [name for _at in sorted(PLACED) for name in PLACED[_at] if name[0] in ("bias", "expert")]
EXPERT_JOBS = [name for _at in sorted(PLACED) for name in PLACED[_at]
               if name[0] in ("x2t", "router", "logits", "gates", "bias", "expert")]

BEFORE_GATES = [name for name in EXPERT_JOBS if name[0] == "expert"][TT - 1]
LAST_JOBS = [name for name in EXPERT_JOBS if name[0] not in ("gates", "bias")]
LAST_JOBS[LAST_JOBS.index(BEFORE_GATES) + 1:LAST_JOBS.index(BEFORE_GATES) + 1] = [("gates",)]
LAST_JOBS[-3:-3] = [("bias", 0), ("bias", 1)]
assert LAST_JOBS[-1] == SUMMED[-1]

JOBS = {PRO: NEXT_JOBS[:6], EPI: [("ot", PAIRS - 1)] + [("wo", ROUNDS - 1, j) for j in range(MT)] + LAST_JOBS}
for _kind in (FIRST, LOOP, LAST):
    JOBS[_kind] = [name for _h in range(HEADS) for _t in range(TT) for name in jobs_of(_kind, _h, _t)]
SPLIT = ("q", "k", "v", "xt", "ot", "x2t")
HI = {kind: [n for n in names if n[0] in SPLIT] for kind, names in JOBS.items()}
BANKS = 3
EXTRA_BANKS = 4
assert len(JOBS[LOOP]) % BANKS == 0


def maximum_at(kind, h, t):
    g, u = (h + 1, t + TT // 2) if t < TT // 2 else (h + 2, t - TT // 2)
    return (g, u) if g < HEADS or kind != LAST else None


def taken_in(kind, h, t):
    names = jobs_of(kind, *((h, t - 1) if t else (h - 1, TT - 1))) if (h, t) != (0, 0) else []
    return names + (jobs_of(kind, h, t) if (h, t) == (HEADS - 1, TT - 1) else [])


class Iteration:

    def __init__(self, kind, b):
        self.kind, self.b = kind, b

    def start(self, lists):
        n = {kind: len(names) for kind, names in lists.items()}
        return {PRO: 0, FIRST: n[PRO], LOOP: (self.b - 1) * n[LOOP] + (n[PRO] + n[FIRST]),
                LAST: n[PRO] + n[FIRST] + (BATCHES - 2) * n[LOOP],
                EPI: n[PRO] + n[FIRST] + (BATCHES - 2) * n[LOOP] + n[LAST]}[self.kind]

    def done(self, lists, name):
        return self.start(lists) + (lists[self.kind].index(name) + 1)

    def done_before(self, lists, name):
        before = {FIRST: PRO, LOOP: LOOP, LAST: LOOP, EPI: LAST}[self.kind]
        return self.start(lists) - (len(lists[before]) - lists[before].index(name) - 1)

    def bank(self, name):
        start = len(JOBS[PRO]) + len(JOBS[FIRST]) if self.kind == LOOP else self.start(JOBS)
        after = self.after_loop(name)
        if after is None:
            return (start + JOBS[self.kind].index(name)) % BANKS
        return (after + BANKS) % (BANKS + EXTRA_BANKS)

    def after_loop(self, name):
        if self.kind != EPI:
            return None
        n = JOBS[EPI].index(name) - min(JOBS[EPI].index(m) for m in JOBS[EPI] if m[0] == "expert")
        return n if n >= 0 else None

    def summed_before(self, name):
        summed = [m for m in JOBS[self.kind] if m in SUMMED]
        return summed[summed.index(name) - 1]

    def free_wait(self, name):
        n, after = self.done(JOBS, name), self.after_loop(name)
        if after is None:
            return n
        reused = n - EXTRA_BANKS
        return reused if after < EXTRA_BANKS else max(reused, n - after + BANKS - 1)


def build(nc, x, kv_t, g_xattn, g_ffn, wq, wk, wv, wo, bo, gate_t, expert_t, expert_b, out):
    x_v = x.rearrange("b (t p) d -> p (b t) d", p=P)
    out_v = out.rearrange("b (t p) d -> p (b t) d", p=P)
    kv_v = kv_t.rearrange("b c k -> c b k")

    ctx = ExitStack()
    with ctx:
        def sb(name, shape, dt=F32):
            return ctx.enter_context(nc.sbuf_tensor(name, shape, dt))

        def bank(name):
            return ctx.enter_context(nc.psum_tensor(name, [P, 512], F32))

        def sem(name):
            return ctx.enter_context(nc.semaphore(name))

        wq_s = sb("wq_s", [P, 2, LC, INNER], F32R)
        wk_s = sb("wk_s", [P, 2, INNER], F32R)
        wv_s = sb("wv_s", [P, 2, INNER], F32R)
        wo_s = sb("wo_s", [P, 2, PAIRS, DIM], F32R)
        ex_s = sb("ex_s", [P, 2, LC, EXPERTS * DIM], F32R)
        gt_s = sb("gt_s", [P, 2, LC, EXPERTS], F32R)
        gt_f = sb("gt_f", [P, LC, EXPERTS])
        eb = sb("eb", [EXPERTS, DIM])
        bo_t = sb("bo_t", [P, DIM])
        gates = sb("gates", [P, 2])
        tg = sb("tg", [P, 2])
        ident = sb("ident", [P, P])
        ident_r = sb("ident_r", [P, P], F32R)
        order = sb("order", [P, EXPERTS])
        minus_half = sb("minus_half", [P, TT])
        ones = sb("ones", [P, 1])
        wv_max = sb("wv_max", [P, 1])
        xin = sb("xin", [P, TT, DIM])
        x2 = sb("x2", [P, TT, DIM])
        xn = sb("xn", [P, TT, DIM])
        kvin = sb("kvin", [P, TOKENS])
        kv_s = sb("kv_s", [P, 2, TOKENS], F32R)
        xt_s = sb("xt_s", [P, 2, LC, TOKENS], F32R)
        v_s = sb("v_s", [P, 2, TT, HEADS, HEAD + 1], F16)
        QA = sb("QA", [P, 4, TOKENS], F32R)
        QB = sb("QB", [P, 4, TOKENS], F32R)
        KA = sb("KA", [P, 4, TOKENS], F32R)
        KB = sb("KB", [P, 4, TOKENS], F32R)
        pf = sb("pf", [P, TT, TOKENS])
        p_s = sb("p_s", [P, 2, 2, TT, TOKENS], F16)
        o_n = sb("o_n", [P, 2, TT, P])
        ot_s = sb("ot_s", [P, 2, GROUP, TOKENS], F32R)
        nmax = sb("nmax", [P, 2, TT], F32R)
        stats = sb("stats", [P, TT, 6])
        mv = sb("mv", [P, TT, 2])
        ve = sb("ve", [P, TT])
        rstd = sb("rstd", [P, TT])
        kmax = sb("kmax", [P, 2])
        v_div = sb("v_div", [P, 1])
        v_mul = sb("v_mul", [P, 1])
        o_mul = sb("o_mul", [P, 1])
        rden = sb("rden", [P, TT])
        x2t_s = sb("x2t_s", [P, 2, LC, TOKENS], F32R)
        acc = sb("acc", [P, TT, DIM])
        logit = sb("logit", [P, TT, EXPERTS])
        prob = sb("prob", [P, TT, EXPERTS])
        r1 = sb("r1", [P, TT])
        r2 = sb("r2", [P, TT])
        m1 = sb("m1", [P, TT, EXPERTS])
        m2 = sb("m2", [P, TT, EXPERTS])
        w1 = sb("w1", [P, TT, EXPERTS])
        p2 = sb("p2", [P, TT, EXPERTS])
        comb = sb("comb", [P, TT, EXPERTS])
        comb_t = xn[0:EXPERTS, :, :].rearrange("p t d -> p (t d)")[:, 0:TOKENS]

        MX = [bank("MX0"), bank("MX1")]
        ST = [bank("ST0"), bank("ST1")]
        MB = [bank(f"MB{n}") for n in range(BANKS)]
        PV = bank("PV")
        SHARED = MB + MX + ST

        flat = p_s[:, :, :, :, :].rearrange("p a b c d -> p (a b c d)").bitcast(F32)
        stage_q = pf[:, :, :].rearrange("p a b -> p (a b)").rearrange("p (c n) -> p c n", c=LC)
        wq_v = wq.rearrange("(c p) n -> p c n", p=P)
        early, rest = slice(0, 2 * P), slice(2 * P, INNER)
        stage_k, stage_v = flat[:, 0:INNER], flat[:, INNER:2 * INNER]
        late_stage = acc[:, :, :].rearrange("p t d -> p (t d)")

        wq_in, wq_rest_in, wk_in, wv_in = sem("wq_in"), sem("wq_rest_in"), sem("wk_in"), sem("wv_in")
        small_in = sem("small_in")
        late_in = [sem("late_in0"), sem("late_in1")]
        w_hi, wq_lo, w_lo = sem("w_hi"), sem("wq_lo"), sem("w_lo")
        late_hi, late_lo = sem("late_hi"), sem("late_lo")
        const_pool, const_dve = sem("const_pool"), sem("const_dve")
        tanh_done = sem("tanh_done")
        x_in, kv_in = sem("x_in"), sem("kv_in")
        x_bias = sem("x_bias")
        ln1_step, ln1_var, ln1_rstd, ln1_done = sem("ln1_step"), sem("ln1_var"), sem("ln1_rstd"), sem("ln1_done")
        ln2_step, ln2_var, ln2_rstd, ln2_done = sem("ln2_step"), sem("ln2_var"), sem("ln2_rstd"), sem("ln2_done")
        kv_hi, kv_lo = sem("kv_hi"), sem("kv_lo")
        kmax_step, kmax_done = sem("kmax_step"), sem("kmax_done")
        scale_done, o_mul_done = sem("scale_done"), sem("o_mul_done")
        job_ready, job_hi, job_free = sem("job_ready"), sem("job_hi"), sem("job_free")
        q_dup = [sem("q_dup0"), sem("q_dup1")]
        k_dup = [sem("k_dup0"), sem("k_dup1")]
        max_ready, max_free = sem("max_ready"), sem("max_free")
        st_ready, st_free = sem("st_ready"), sem("st_free")
        p_hi, p_lo = sem("p_hi"), sem("p_lo")
        pv_ready, den_ready, o_ready = sem("pv_ready"), sem("den_ready"), sem("o_ready")
        lg_shift, lg_exp, comb_ready = sem("lg_shift"), sem("lg_exp"), sem("comb_ready")
        gate_step, sum_step = sem("gate_step"), sem("sum_step")
        y_out = sem("y_out")
        block = ctx.enter_context(nc.Block())

        def tile_count(b, h, t):
            return b * (HEADS * TT) + (h * TT + t + 1)

        def st_unit(b, h, t):
            last = isinstance(b, int) and (b, h) == (BATCHES - 1, HEADS - 1)
            return h * (TT + 1) + (t if t < ROW_UNIT or last else t + 1)

        def st_count(b, h, t):
            return b * (HEADS * (TT + 1)) + (st_unit(b, h, t) + 2)

        def st_bank(b, h, t):
            return ST[(st_unit(b, h, t) + 1) % 2]

        def row_unit(h):
            return (h - 1) * (TT + 1) + ROW_UNIT

        def row_count(b, h):
            if h == 0 and isinstance(b, int) and b == 0:
                return 1
            return b * (HEADS * (TT + 1)) + (row_unit(h) + 2)

        def row_bank(h):
            return ST[(row_unit(h) + 1) % 2]

        def head_count(b, h):
            return b * HEADS + (h + 1)

        def dup_count(b, p):
            return 16 * (b * (PAIRS // 2) + (p // 2 + 1))

        late = [(wo[256 * k:256 * (k + 1), :].rearrange("(c p) n -> p c n", p=P),
                 wo_s[:, 0, 2 * k:2 * k + 2, :], wo_s[:, 1, 2 * k:2 * k + 2, :]) for k in range(PAIRS // 2)]
        late += [(expert_t[P * c:P * (c + 1), 512 * k:512 * (k + 1)],
                  ex_s[:, 0, c, 512 * k:512 * (k + 1)], ex_s[:, 1, c, 512 * k:512 * (k + 1)])
                 for c in range(LC) for k in range(EC)]

        def late_raw(n):
            raw = late_stage[:, 512 * (n % 2):512 * (n % 2 + 1)]
            return raw.rearrange("p (c n) -> p c n", c=2) if n < PAIRS // 2 else raw

        CONST_POOL = EXPERTS + 5
        CONST_DVE = 4

        def run(engine, step=None, slot=None, before=None, after=None):
            def turn(it):
                if before:
                    before(it)
                for h in range(HEADS):
                    if step:
                        step(it, h)
                    for t in range(TT if slot else 0):
                        slot(it, h, t)
                if after:
                    after(it)
            turn(Iteration(FIRST, 0))
            with engine.Fori(1, BATCHES - 1) as b:
                turn(Iteration(LOOP, b))
            turn(Iteration(LAST, BATCHES - 1))

        @block.sync
        def _(sp):
            sp.dma_start(xin[:, :, :], x_v[:, 0:TT, :]).then_inc(x_in, 16)
            sp.dma_start(kvin[:, :], kv_v[:, 0, :]).then_inc(kv_in, 16)
            sp.dma_start(stage_q[:, :, early], wq_v[:, :, early]).then_inc(wq_in, 16)
            sp.dma_start(stage_k, wk).then_inc(wk_in, 16)
            sp.dma_start(stage_q[:, :, rest], wq_v[:, :, rest]).then_inc(wq_rest_in, 16)
            sp.dma_start(stage_v, wv).then_inc(wv_in, 16)
            sp.dma_start(gates[:, 0:1], g_xattn.partition_broadcast(P)).then_inc(small_in, 16)
            sp.dma_start(gates[:, 1:2], g_ffn.partition_broadcast(P)).then_inc(small_in, 16)
            sp.dma_start(bo_t[:, :], bo.partition_broadcast(P)).then_inc(small_in, 16)
            sp.dma_start(eb[:, :], expert_b).then_inc(small_in, 16)
            sp.dma_start(gt_f[:, :, :], gate_t.rearrange("(c p) e -> p c e", p=P)).then_inc(small_in, 16)

            def copy(it, name):
                kind, p = name
                heads = slice(2 * (p % 2), 2 * (p % 2) + 2)
                dst, src, copied = ((QB[0:HEAD, heads, :], QA[0:HEAD, heads, :], q_dup) if kind == "q" else
                                    (KA[HEAD:P, heads, :], KA[0:HEAD, heads, :], k_dup))
                sp.wait_ge(job_hi, it.done(HI, name))
                sp.dma_start(dst.bitcast(F32), src.bitcast(F32)).then_inc(copied[p % 2], 16)

            for name in [name for name in JOBS[PRO] if name[0] in "qk"]:
                copy(Iteration(PRO, 0), name)

            def before(it):
                if it.kind != LAST:
                    sp.wait_ge(kmax_step, it.b + 1)
                    sp.wait_ge(kv_hi, it.b + 1)
                    sp.wait_ge(kv_lo, it.b + 1)
                    sp.dma_start(kvin[:, :], kv_v[:, bass.ds(it.b + 1, 1), :].rearrange("c a k -> c (a k)"))\
                      .then_inc(kv_in, 16)

            def step(it, h):
                if it.kind == FIRST and h < len(late):
                    if h >= 2:
                        sp.wait_ge(late_lo, h - 1)
                    sp.dma_start(late_raw(h), late[h][0]).then_inc(late_in[h % 2], 16)
                for t in range(TT):
                    for name in jobs_of(it.kind, h, t):
                        if name[0] in "qk":
                            copy(it, name)
                if h == 5 and it.kind != LAST:
                    sp.wait_ge(ln1_done, it.b + 1)
                    sp.wait_ge(x_bias, it.b + 1)
                    sp.dma_start(xin[:, :, :], x_v[:, bass.ds(it.b * TT + TT, TT), :]).then_inc(x_in, 16)

            def after(it):
                if it.kind != FIRST:
                    store(it)

            def store(it):
                m = it.b - 1
                sp.wait_ge(job_free, it.done(JOBS, SUMMED[-1]) + BANKS)
                sp.dma_start(out_v[:, bass.ds(m * TT, TT), :], acc[:, :, :]).then_inc(y_out, 16)

            run(sp, step, before=before, after=after)
            store(Iteration(EPI, BATCHES))
            sp.wait_ge(y_out, 16 * BATCHES + 16)

        @block.gpsimd
        def _(pool):
            pool.memset(ident[:, :], 0.0).then_inc(const_pool, 1)
            for e in range(EXPERTS):
                pool.memset(order[:, e:e + 1], float(EXPERTS - e)).then_inc(const_pool, 1)
            pool.memset(minus_half[:, :], -0.5).then_inc(const_pool, 1)
            pool.memset(v_s[:, 0, :, :, HEAD:HEAD + 1], 1.0).then_inc(const_pool, 1)
            pool.memset(v_s[:, 1, :, :, HEAD:HEAD + 1], 0.0).then_inc(const_pool, 1)
            pool.wait_ge(const_pool, EXPERTS + 4)
            pool.affine_select(out=ident[:, :], in_=ident[:, :], compare_op=ALU.not_equal, fill=1.0, base=0,
                               pattern=[[-1, P]], channel_multiplier=1).then_inc(const_pool, 1)

            def power(n, var, rstd_done):
                pool.wait_ge(var, n)
                pool.tensor_tensor(rstd[:, :], ve[:, :], minus_half[:, :], ALU.pow).then_inc(rstd_done, 1)

            power(1, ln1_var, ln1_rstd)
            pool.wait_ge(w_hi, 2)
            pool.tensor_tensor(wk_s[:, 1, :], stage_k, wk_s[:, 0, :].bitcast(F32), ALU.subtract).then_inc(w_lo, 1)
            pool.wait_ge(w_hi, 3)
            pool.tensor_tensor(wv_s[:, 1, :], stage_v, wv_s[:, 0, :].bitcast(F32), ALU.subtract).then_inc(w_lo, 1)
            pool.wait_ge(w_hi, 5)
            pool.tensor_tensor(gt_s[:, 1, :, :], gt_f[:, :, :], gt_s[:, 0, :, :].bitcast(F32), ALU.subtract)\
                .then_inc(w_lo, 1)

            def step(it, h):
                for t in range(TT):
                    pool.wait_ge(p_hi, tile_count(it.b, h, t))
                    pool.tensor_tensor(p_s[:, h % 2, 1, t, :], pf[:, t, :], p_s[:, h % 2, 0, t, :], ALU.subtract)\
                        .then_inc(p_lo, 1)
                    if (h, t) == LN2_POWER_AT and it.kind != FIRST:
                        power(it.b, ln2_var, ln2_rstd)
                if h == 3:
                    pool.wait_ge(x_in, 16 * it.b + 16)
                    if it.kind == FIRST:
                        pool.wait_ge(const_dve, CONST_DVE)
                    else:
                        pool.wait_ge(job_free, it.done(JOBS, ("wo", ROUNDS - 1, MT - 1)) + BANKS)
                    pool.tensor_tensor(x2[:, :, :], xin[:, :, :],
                                       bo_t[:, :].unsqueeze(1).broadcast_to([P, TT, DIM]), ALU.add)\
                        .then_inc(x_bias, 1)
                if h == 10 and it.kind != LAST:
                    power(it.b + 2, ln1_var, ln1_rstd)

            run(pool, step)
            power(BATCHES, ln2_var, ln2_rstd)

        @block.scalar
        def _(act):
            act.wait_ge(kv_in, 16)
            act.activation(kv_s[:, 0, :], kvin[:, :], ACT.Copy).then_inc(kv_hi, 1)
            act.wait_ge(wq_in, 16)
            act.activation(wq_s[:, 0, :, early], stage_q[:, :, early], ACT.Copy).then_inc(w_hi, 1)
            act.wait_ge(wk_in, 16)
            act.activation(wk_s[:, 0, :], stage_k, ACT.Copy).then_inc(w_hi, 1)
            def take_hi(it, name):
                act.wait_ge(job_ready, it.done(JOBS, name))
                m = SHARED[it.bank(name)]
                kind = name[0]
                if kind in ("q", "k"):
                    dst, s = (QA if kind == "q" else KA), 2 * (name[1] % 2)
                    act.activation(dst[0:HEAD, s, :], m[0:HEAD, :], ACT.Copy)
                    last = act.activation(dst[0:HEAD, s + 1, :], m[HEAD:P, :], ACT.Copy)
                elif kind == "xt":
                    last = act.activation(xt_s[:, 0, name[1], :], m[:, :], ACT.Copy)
                elif kind == "x2t":
                    last = act.activation(x2t_s[:, 0, name[1], :], m[:, :], ACT.Copy)
                elif kind == "ot":
                    last = act.activation(ot_s[:, 0, name[1] % GROUP, :], m[:, :], ACT.Copy)
                else:
                    t, g = name[1:3]
                    act.wait_ge(scale_done, it.b + 1 if g or len(name) > 3 else it.b + 2)
                    last = act.activation(v_s[:, 0, t, g * HH:(g + 1) * HH, 0:HEAD],
                                          m[:, :].rearrange("p (h d) -> p h d", d=HEAD), ACT.Copy,
                                          scale=v_mul[:, 0:1])
                last.then_inc(job_hi, 1)

            def take_row(b, h):
                act.wait_ge(st_ready, row_count(b, h))
                act.activation(QB[HEAD:HEAD + 1, h % 4, :], row_bank(h)[HEAD:HEAD + 1, :], ACT.Copy)\
                   .then_inc(st_free, 1)

            pro = Iteration(PRO, 0)
            for name in HI[PRO]:
                if name == ("q", 0):
                    act.wait_ge(wv_in, 16)
                    act.activation(wv_s[:, 0, :], stage_v, ACT.Copy).then_inc(w_hi, 1)
                    act.wait_ge(wq_rest_in, 16)
                    act.activation(wq_s[:, 0, :, rest], stage_q[:, :, rest], ACT.Copy).then_inc(w_hi, 1)
                    act.wait_ge(small_in, 5 * 16)
                    act.activation(gt_s[:, 0, :, :], gt_f[:, :, :], ACT.Copy).then_inc(w_hi, 1)
                    act.activation(tg[:, :], gates[:, :], ACT.Tanh).then_inc(tanh_done, 1)
                take_hi(pro, name)
            take_row(0, 0)
            act.wait_ge(wq_lo, 2)
            act.wait_ge(w_lo, 2)

            def slot(it, h, t):
                b, kind = it.b, it.kind
                if (h, t) == KV_HI_AT and kind != LAST:
                    act.wait_ge(kv_in, 16 * b + 32)
                    act.wait_ge(job_ready, it.done(JOBS, ("k", PAIRS - 1)))
                    act.activation(kv_s[:, 0, :], kvin[:, :], ACT.Copy).then_inc(kv_hi, 1)
                for part in ACT_ORDER[h % 2][t].split():
                    if part == "hi":
                        for name in taken_in(kind, h, t):
                            if name[0] in SPLIT:
                                take_hi(it, name)
                    elif part == "exp":
                        if t == ROW_UNIT and (h + 1 < HEADS or kind != LAST):
                            take_row(b, h + 1)
                        act.wait_ge(st_ready, st_count(b, h, t))
                        act.wait_ge(p_lo, tile_count(b, h - 1, t) + TT)
                        act.activation(pf[:, t, :], st_bank(b, h, t)[:, :], ACT.Exp, bias=P_SHIFT, scale=SCALE)\
                           .then_inc(st_free, 1)
                    elif part == "copy":
                        if t:
                            probabilities(b, h, t - 1)
                        elif h or kind != FIRST:
                            probabilities(b, h - 1, TT - 1)
                if kind != FIRST and (h, t) == LOGITS_AT:
                    logit_exp(b - 1)
                if kind == FIRST and t == TT - 1 and h < len(late):
                    act.wait_ge(late_in[h % 2], 16 * (h // 2 + 1))
                    act.activation(late[h][1], late_raw(h), ACT.Copy).then_inc(late_hi, 1)

            def probabilities(b, h, t):
                act.wait_ge(st_free, st_count(b, h, t) + 2)
                if t == 0:
                    act.wait_ge(pv_ready, head_count(b, h - 2) + 2)
                act.activation(p_s[:, h % 2, 0, t, :], pf[:, t, :], ACT.Copy).then_inc(p_hi, 1)

            def logit_exp(m):
                act.wait_ge(lg_shift, m + 1)
                act.activation(prob[:, :, :], logit[:, :, :], ACT.Exp).then_inc(lg_exp, 1)

            run(act, slot=slot)
            probabilities(BATCHES - 1, HEADS - 1, TT - 1)
            for name in HI[EPI]:
                take_hi(Iteration(EPI, BATCHES), name)
            logit_exp(BATCHES - 1)

        @block.vector
        def _(dve):
            dve.memset(ones[:, :], 1.0).then_inc(job_free, BANKS)
            dve.memset(rden[:, :], 0.0).then_inc(max_free, 2)
            dve.memset(r1[:, :], 0.0).then_inc(st_free, 2)
            dve.memset(r2[:, :], 0.0).then_inc(p_lo, TT)
            dve.memset(ve[:, :], 0.0).then_inc(pv_ready, 2)
            dve.memset(rstd[:, :], 0.0).then_inc(o_ready, 1)
            dve.memset(p2[:, :, :], 0.0).then_inc(y_out, 16)
            dve.memset(KB[HEAD:HEAD + 1, :, :].bitcast(F32), 1.0).then_inc(const_dve, 1)

            def statistics(src, n, count, var):
                for t in range(TT):
                    last = dve.bn_stats(stats[:, t, :], src[:, t, :])
                last.then_inc(n, 1)
                dve.wait_ge(n, count)
                dve.memset(ve[:, :], 0.0)
                for t in range(TT):
                    last = dve.bn_aggr(mv[:, t, :], stats[:, t, :])
                last.then_inc(n, 1)
                dve.wait_ge(n, count + 1)
                dve.tensor_scalar(ve[:, :], mv[:, :, 1], EPS, None, ALU.add).then_inc(var, 1)

            def apply(src, rstd_done, count, done):
                dve.wait_ge(rstd_done, count)
                for t in range(TT):
                    last = dve.tensor_scalar(xn[:, t, :], src[:, t, :], mv[:, t, 0:1], rstd[:, t:t + 1],
                                             ALU.subtract, ALU.mult)
                last.then_inc(done, 1)

            def bound(b):
                dve.wait_ge(kv_in, 16 * b + 16)
                dve.tensor_reduce(kmax[:, 0:1], kvin[:, :], AX.X, ALU.max, apply_absolute_value=True)\
                   .then_inc(kmax_step, 1)
                dve.wait_ge(kmax_step, b + 1)
                dve.tensor_tensor(kmax[:, 1:2], kmax[:, 0:1], wv_max[:, :], ALU.mult).then_inc(kmax_done, 1)

            def context_lo(b):
                dve.wait_ge(kv_hi, b + 1)
                dve.tensor_tensor(kv_s[:, 1, :], kvin[:, :], kv_s[:, 0, :].bitcast(F32), ALU.subtract)\
                   .then_inc(kv_lo, 1)

            def take(it, name):
                m = SHARED[it.bank(name)]
                kind = name[0]
                if kind not in SPLIT:
                    dve.wait_ge(job_ready, it.done(JOBS, name))
                if kind == "wo":
                    _, r, j = name
                    if r == 0:
                        dve.wait_ge(x_bias, it.b + 1)
                    if r == ROUNDS - 1:
                        dve.wait_ge(late_lo, len(late))
                        dve.wait_ge(y_out, 16 * it.b)
                    dst = acc if r == ROUNDS - 1 else x2
                    last = dve.scalar_tensor_tensor(dst[:, 2 * j:2 * j + 2, :],
                                                    m[:, :].rearrange("p (a n) -> p a n", a=2),
                                                    tg[:, 0:1], x2[:, 2 * j:2 * j + 2, :], ALU.mult, ALU.add)
                elif kind == "bound":
                    last = dve.tensor_scalar(v_div[:, :], m[:, 0:1], 1.0 / V_RANGE, 1e-30, ALU.mult, ALU.max)
                elif kind in ("router", "gates"):
                    last = dve.tensor_copy(comb_t, m[0:EXPERTS, :])
                elif kind == "logits":
                    last = dve.tensor_copy(m1[:, :, :], m[:, 0:TT * EXPERTS].rearrange("p (t e) -> p t e", t=TT))
                elif kind == "bias":
                    j = name[1]
                    dve.wait_ge(job_free, it.done(JOBS, it.summed_before(name)) + BANKS)
                    last = dve.tensor_tensor(acc[:, 2 * j:2 * j + 2, :], m[:, :].rearrange("p (a n) -> p a n", a=2),
                                             acc[:, 2 * j:2 * j + 2, :], ALU.add)
                elif kind == "expert":
                    _, t, e = name
                    if (t, e) == (0, 0):
                        dve.wait_ge(comb_ready, it.b)
                    else:
                        dve.wait_ge(job_free, it.done(JOBS, it.summed_before(name)) + BANKS)
                    for i in range(2):
                        last = dve.scalar_tensor_tensor(acc[:, t, :], m[:, DIM * i:DIM * (i + 1)],
                                                        comb[:, t, 2 * e + i:2 * e + i + 1], acc[:, t, :],
                                                        ALU.mult, ALU.add)
                        if i == 0:
                            last.then_inc(sum_step, 1)
                            dve.wait_ge(sum_step, (it.b - 1) * (TT * EC) + (t * EC + e + 1))
                if kind not in SPLIT:
                    last.then_inc(job_free, 1)
                    if kind == "bound":
                        dve.wait_ge(job_free, it.done(JOBS, name) + BANKS)
                        dve.reciprocal(v_mul[:, :], v_div[:, :]).then_inc(scale_done, 1)
                        dve.wait_ge(scale_done, 1 if it.kind == PRO else it.b + 2)
                    return
                dve.wait_ge(job_hi, it.done(HI, name))
                if kind == "q":
                    s = 2 * (name[1] % 2)
                    for i in range(2):
                        last = dve.tensor_tensor(QA[HEAD:P, s + i, :], m[HEAD * i:HEAD * i + HEAD, :],
                                                 QA[0:HEAD, s + i, :].bitcast(F32), ALU.subtract)
                elif kind == "k":
                    s = 2 * (name[1] % 2)
                    for i in range(2):
                        last = dve.tensor_tensor(KB[0:HEAD, s + i, :], m[HEAD * i:HEAD * i + HEAD, :],
                                                 KA[0:HEAD, s + i, :].bitcast(F32), ALU.subtract)
                elif kind == "xt":
                    last = dve.tensor_tensor(xt_s[:, 1, name[1], :], m[:, :], xt_s[:, 0, name[1], :].bitcast(F32),
                                             ALU.subtract)
                elif kind == "x2t":
                    last = dve.tensor_tensor(x2t_s[:, 1, name[1], :], m[:, :], x2t_s[:, 0, name[1], :].bitcast(F32),
                                             ALU.subtract)
                elif kind == "ot":
                    s = name[1] % GROUP
                    last = dve.tensor_tensor(ot_s[:, 1, s, :], m[:, :], ot_s[:, 0, s, :].bitcast(F32), ALU.subtract)
                else:
                    t, g = name[1:3]
                    last = dve.scalar_tensor_tensor(v_s[:, 1, t, g * HH:(g + 1) * HH, 0:HEAD],
                                                    m[:, :].rearrange("p (h d) -> p h d", d=HEAD), v_mul[:, 0:1],
                                                    v_s[:, 0, t, g * HH:(g + 1) * HH, 0:HEAD],
                                                    ALU.mult, ALU.subtract)
                last.then_inc(job_free, 1)

            def maximum(b, h, t):
                dve.wait_ge(max_ready, tile_count(b, h, t))
                dve.tensor_reduce(nmax[:, h % 2, t:t + 1], MX[t % 2][:, :], AX.X, ALU.max, negate=True)\
                   .then_inc(max_free, 1)

            def normalise(b, h):
                heads = PV[:, 0:TT * (HEAD + 1)].rearrange("p (t d) -> p t d", t=TT)
                dve.wait_ge(pv_ready, head_count(b, h) + 2)
                dve.reciprocal(rden[:, :], heads[:, :, HEAD]).then_inc(den_ready, 1)
                dve.wait_ge(den_ready, head_count(b, h))
                side, col = h % HEADS // 2 % 2, HEAD * (h % 2)
                dve.scalar_tensor_tensor(o_n[:, side, :, col:col + HEAD], heads[:, :, 0:HEAD], o_mul[:, 0:1],
                                         rden[:, :].unsqueeze(2).broadcast_to([P, TT, HEAD]),
                                         ALU.mult, ALU.mult).then_inc(o_ready, 1)

            dve.wait_ge(x_in, 16)
            statistics(xin, ln1_step, 1, ln1_var)
            context_lo(0)
            apply(xin, ln1_rstd, 1, ln1_done)
            dve.wait_ge(w_hi, 1)
            dve.tensor_tensor(wq_s[:, 1, :, early], stage_q[:, :, early], wq_s[:, 0, :, early].bitcast(F32),
                              ALU.subtract).then_inc(wq_lo, 1)
            pro = Iteration(PRO, 0)
            for name in JOBS[PRO]:
                if name == ("q", 0):
                    dve.wait_ge(wv_in, 16)
                    dve.tensor_reduce(wv_max[:, :], stage_v, AX.X, ALU.max, apply_absolute_value=True)\
                       .then_inc(const_dve, 1)
                    dve.wait_ge(const_dve, 2)
                    bound(0)
                    dve.wait_ge(const_pool, CONST_POOL)
                    dve.tensor_copy(ident_r[:, :], ident[:, :]).then_inc(const_dve, 1)
                if name == ("q", 1):
                    for t in range(TT):
                        maximum(0, 0, t)
                    dve.wait_ge(w_hi, 4)
                    dve.tensor_tensor(wq_s[:, 1, :, rest], stage_q[:, :, rest], wq_s[:, 0, :, rest].bitcast(F32),
                                      ALU.subtract).then_inc(wq_lo, 1)
                if name == ("bound",):
                    dve.wait_ge(tanh_done, 1)
                    dve.tensor_scalar(bo_t[:, :], bo_t[:, :], tg[:, 0:1], None, ALU.mult).then_inc(const_dve, 1)
                take(pro, name)
            for t in range(TT // 2):
                maximum(0, 1, t)

            def outputs_scale(b):
                dve.wait_ge(scale_done, b + 1)
                dve.tensor_copy(o_mul[:, :], v_div[:, :]).then_inc(o_mul_done, 1)
                dve.wait_ge(o_mul_done, b + 1)

            def slot(it, h, t):
                b, kind = it.b, it.kind
                taken = taken_in(kind, h, t)
                first_split = min([n for n, name in enumerate(taken) if name[0] in SPLIT], default=len(taken))
                for part in DVE_ORDER[h % 2][t].split():
                    if part == "normalise":
                        if t == NORMALISE_SLOT and (h >= VALUES_BACK or kind != FIRST):
                            if h == VALUES_BACK:
                                outputs_scale(b)
                            normalise(b, h - VALUES_BACK)
                    elif part == "whole":
                        for name in taken[:first_split]:
                            take(it, name)
                    elif part == "maximum":
                        if maximum_at(kind, h, t):
                            maximum(b, *maximum_at(kind, h, t))
                    elif part == "lo":
                        for name in taken[first_split:]:
                            take(it, name)
                if kind == FIRST and t == 1 and 1 <= h <= len(late):
                    dve.wait_ge(late_hi, h)
                    dve.tensor_tensor(late[h - 1][2], late_raw(h - 1), late[h - 1][1].bitcast(F32), ALU.subtract)\
                       .then_inc(late_lo, 1)
                if ("logits",) in taken:
                    route(it, 0)
                if kind != FIRST:
                    if (h, t) in ROUTE_SLOTS:
                        route(it, 1 + ROUTE_SLOTS.index((h, t)))
                    if (h, t) == LN2_AT:
                        dve.wait_ge(job_free, it.done(JOBS, ("wo", ROUNDS - 1, MT - 1)) + BANKS)
                        second_norm(b - 1)
                    if (h, t) == LN2_APPLY_AT:
                        apply(acc, ln2_rstd, b, ln2_done)
                if kind != LAST:
                    if (h, t) == BOUND_AT:
                        bound(b + 1)
                    if (h, t) == LN1_AT:
                        dve.wait_ge(x_in, 16 * b + 32)
                        statistics(xin, ln1_step, 2 * b + 3, ln1_var)
                    if (h, t) == LN1_APPLY_AT:
                        apply(xin, ln1_rstd, b + 2, ln1_done)
                    if (h, t) == KV_LO_AT:
                        context_lo(b + 1)

            def second_norm(m):
                statistics(acc, ln2_step, 2 * m + 1, ln2_var)

            GATE_STEPS = 17

            def over(v):
                return v[:, :].unsqueeze(2).broadcast_to([P, TT, EXPERTS])

            def route(it, part):
                m = it.b - 1
                n = [(0, 1, 4, 7, 10, 13, 16)[part]]

                def then(ins):
                    n[0] += 1
                    ins.then_inc(gate_step, 1)
                    dve.wait_ge(gate_step, m * GATE_STEPS + n[0])

                def candidates(src):
                    then(dve.tensor_reduce(r1[:, :], src[:, :, :], AX.X, ALU.max))
                    then(dve.tensor_tensor(w1[:, :, :], src[:, :, :], over(r1), ALU.is_equal))
                    then(dve.tensor_tensor(w1[:, :, :], w1[:, :, :],
                                           order[:, :].unsqueeze(1).broadcast_to([P, TT, EXPERTS]), ALU.mult))

                def first(mask):
                    then(dve.tensor_reduce(r1[:, :], w1[:, :, :], AX.X, ALU.max))
                    then(dve.tensor_tensor(mask[:, :, :], w1[:, :, :], over(r1), ALU.is_equal))

                if part == 0:
                    dve.wait_ge(job_free, it.done(JOBS, ("logits",)) + BANKS)
                    then(dve.tensor_reduce(r1[:, :], m1[:, :, :], AX.X, ALU.max, negate=True))
                    dve.tensor_tensor(logit[:, :, :], m1[:, :, :], over(r1), ALU.add).then_inc(lg_shift, 1)
                elif part == 1:
                    dve.wait_ge(lg_exp, m + 1)
                    then(dve.tensor_reduce(r1[:, :], prob[:, :, :], AX.X, ALU.add))
                    then(dve.reciprocal(r2[:, :], r1[:, :]))
                    then(dve.tensor_tensor(prob[:, :, :], prob[:, :, :], over(r2), ALU.mult))
                elif part == 2:
                    candidates(prob)
                elif part == 3:
                    first(m1)
                    then(dve.scalar_tensor_tensor(p2[:, :, :], m1[:, :, :], -2.0, prob[:, :, :], ALU.mult, ALU.add))
                elif part == 4:
                    candidates(p2)
                elif part == 5:
                    first(m2)
                    then(dve.tensor_tensor(m2[:, :, :], m1[:, :, :], m2[:, :, :], ALU.add))
                else:
                    then(dve.tensor_tensor(m2[:, :, :], prob[:, :, :], m2[:, :, :], ALU.mult))
                    assert n[0] == GATE_STEPS
                    dve.tensor_scalar(comb[:, :, :], m2[:, :, :], tg[:, 1:2], None, ALU.mult).then_inc(comb_ready, 1)

            run(dve, slot=slot)
            epi = Iteration(EPI, BATCHES)
            normalise(BATCHES - 1, HEADS - 2)
            normalise(BATCHES - 1, HEADS - 1)
            for name in JOBS[EPI]:
                take(epi, name)
                if name == ("wo", ROUNDS - 1, MT - 1):
                    dve.wait_ge(job_free, epi.done(JOBS, name) + BANKS)
                    second_norm(BATCHES - 1)
                    apply(acc, ln2_rstd, BATCHES, ln2_done)
                if name == ("logits",):
                    for part in range(1 + len(ROUTE_SLOTS)):
                        route(epi, part)

        @block.tensor
        def _(pe):
            def parts(dst, terms):
                n = 3 * len(terms)
                k = 0
                for (s_hi, s_lo), (m_hi, m_lo) in terms:
                    for s, m in ((s_hi, m_hi), (s_hi, m_lo), (s_lo, m_hi)):
                        last = pe.matmul(dst, s, m, start=(k == 0), stop=(k == n - 1))
                        k += 1
                return last

            def tile(t):
                return slice(t * P, (t + 1) * P)

            def turned(bank_, src):
                for t in range(TT):
                    last = pe.transpose(bank_[:, tile(t)], src(t), ident[:, :])
                return last

            def produce(it, name):
                kind = name[0]
                m = SHARED[it.bank(name)]
                if kind == "xt":
                    pe.wait_ge(ln1_done, it.b + 1 if it.kind == PRO else it.b + 2)
                elif kind == "ot":
                    p = name[1]
                    if p == PAIRS - 1:
                        pe.wait_ge(o_ready, head_count(it.b, -1) + 1)
                    else:
                        pe.wait_ge(o_ready, head_count(it.b, 2 * p + 1) + 1)
                elif kind == "wo":
                    pe.wait_ge(job_free, it.done(JOBS, ("ot", name[1] * GROUP + GROUP - 1)) + BANKS)
                    if it.kind == FIRST:
                        pe.wait_ge(late_lo, PAIRS // 2)
                elif kind == "k" and it.kind != PRO and name[1] == 0:
                    pe.wait_ge(kv_lo, it.b + 2)
                elif kind == "q" and it.kind == FIRST and name[1] == 2:
                    pe.wait_ge(wq_lo, 2)
                elif kind == "v" and it.kind == FIRST and name[1] == 0:
                    pe.wait_ge(w_lo, 2)
                elif kind == "bound":
                    pe.wait_ge(kmax_done, 1 if it.kind == PRO else it.b + 2)
                elif kind == "x2t":
                    pe.wait_ge(ln2_done, it.b)
                elif kind in ("router", "logits"):
                    before = {"router": ("x2t", LC - 1), "logits": ("router",)}[kind]
                    pe.wait_ge(job_free, it.done(JOBS, before) + BANKS)
                elif kind == "gates":
                    pe.wait_ge(comb_ready, it.b)
                elif kind == "bias":
                    pe.wait_ge(job_free, it.done(JOBS, ("gates",)) + BANKS)
                elif kind == "q" and it.kind != PRO and name[1] == 0:
                    pe.wait_ge(job_free, it.done(JOBS, ("xt", LC - 1)) + BANKS)
                pe.wait_ge(job_free, it.free_wait(name))
                if kind == "xt":
                    c = name[1]
                    last = turned(m, lambda t: xn[:, t, c * P:(c + 1) * P])
                elif kind == "q":
                    cols = slice(name[1] * P, (name[1] + 1) * P)
                    last = parts(m[:, :], [((wq_s[:, 0, c, cols], wq_s[:, 1, c, cols]),
                                            (xt_s[:, 0, c, :], xt_s[:, 1, c, :])) for c in range(LC)])
                elif kind == "k":
                    cols = slice(name[1] * P, (name[1] + 1) * P)
                    last = parts(m[:, :], [((wk_s[:, 0, cols], wk_s[:, 1, cols]), (kv_s[:, 0, :], kv_s[:, 1, :]))])
                elif kind == "v":
                    t, g = name[1:3]
                    cols = slice(g * 512, (g + 1) * 512)
                    last = parts(m[:, :], [((kv_s[:, 0, tile(t)], kv_s[:, 1, tile(t)]),
                                            (wv_s[:, 0, cols], wv_s[:, 1, cols]))])
                elif kind == "bound":
                    last = pe.matmul(m[:, 0:1], kmax[:, 1:2].broadcast_to([P, P]), ones[:, :], start=True, stop=True)
                elif kind == "x2t":
                    last = turned(m, lambda t: xn[:, t, name[1] * P:(name[1] + 1) * P])
                elif kind == "router":
                    last = parts(m[0:EXPERTS, :], [((gt_s[:, 0, c, :], gt_s[:, 1, c, :]),
                                                    (x2t_s[:, 0, c, :], x2t_s[:, 1, c, :])) for c in range(LC)])
                elif kind == "logits":
                    for t in range(TT):
                        last = pe.matmul(m[:, t * EXPERTS:(t + 1) * EXPERTS], comb_t[:, tile(t)],
                                         ident[0:EXPERTS, 0:EXPERTS], start=True, stop=True)
                elif kind == "gates":
                    for t in range(TT):
                        last = pe.transpose(m[0:EXPERTS, tile(t)], comb[:, t, :], ident[:, :])
                elif kind == "bias":
                    for i in range(2):
                        last = pe.matmul(m[:, DIM * i:DIM * (i + 1)], comb_t[:, tile(2 * name[1] + i)],
                                         eb[:, :], start=True, stop=True)
                elif kind == "expert":
                    _, t, e = name
                    cols = slice(e * 512, (e + 1) * 512)
                    last = parts(m[:, :], [((x2t_s[:, 0, c, tile(t)], x2t_s[:, 1, c, tile(t)]),
                                            (ex_s[:, 0, c, cols], ex_s[:, 1, c, cols])) for c in range(LC)])
                elif kind == "ot":
                    last = turned(m, lambda t: o_n[:, name[1] % 2, t, :])
                else:
                    _, r, j = name
                    for i in range(2):
                        q = tile(2 * j + i)
                        last = parts(m[:, DIM * i:DIM * (i + 1)],
                                     [((ot_s[:, 0, k, q], ot_s[:, 1, k, q]),
                                       (wo_s[:, 0, r * GROUP + k, :], wo_s[:, 1, r * GROUP + k, :]))
                                      for k in range(GROUP)])
                last.then_inc(job_ready, 1)

            def maximum(b, h, t):
                s = h % 4
                pe.wait_ge(max_free, tile_count(b, h, t))
                pe.matmul(MX[t % 2][:, :], QA[0:HEAD, s, tile(t)], KA[0:HEAD, s, :], start=True, stop=True)\
                  .then_inc(max_ready, 1)

            def row(b, h):
                pe.wait_ge(max_free, tile_count(b, h, TT - 1) + 2)
                pe.wait_ge(st_free, row_count(b, h))
                for t in range(TT):
                    last = pe.matmul(row_bank(h)[:, tile(t)], nmax[:, h % 2, t:t + 1].broadcast_to([P, P]),
                                     ident_r[:, :], start=True, stop=True)
                last.then_inc(st_ready, 1)

            def scores(b, h, t):
                s = h % 4
                pe.wait_ge(st_free, st_count(b, h, t))
                pe.matmul(st_bank(b, h, t)[:, :], KA[:, s, tile(t)], QA[:, s, :], start=True, stop=False)
                pe.matmul(st_bank(b, h, t)[:, :], KB[0:HEAD + 1, s, tile(t)], QB[0:HEAD + 1, s, :],
                          start=False, stop=True).then_inc(st_ready, 1)

            def values(b, h):
                pe.wait_ge(p_lo, tile_count(b, h, TT - 1) + TT)
                pe.wait_ge(o_ready, head_count(b, h))
                for t in range(TT):
                    for k in range(TT):
                        for n, (i, j) in enumerate(((0, 0), (0, 1), (1, 0))):
                            last = pe.matmul(PV[:, t * (HEAD + 1):(t + 1) * (HEAD + 1)],
                                             p_s[:, h % 2, i, k, tile(t)], v_s[:, j, k, h % HEADS, :],
                                             start=(k == 0 and n == 0), stop=(k == TT - 1 and n == 2))
                last.then_inc(pv_ready, 1)

            pe.wait_ge(const_pool, EXPERTS + 5)
            pro = Iteration(PRO, 0)
            for name in JOBS[PRO]:
                if name == ("q", 0):
                    pe.wait_ge(wq_lo, 1)
                    pe.wait_ge(job_free, pro.done(JOBS, ("xt", LC - 1)) + BANKS)
                    pe.wait_ge(kv_lo, 1)
                if name == ("k", 0):
                    pe.wait_ge(w_lo, 1)
                if name == ("q", 1):
                    pe.wait_ge(job_hi, pro.done(HI, ("k", 0)))
                    for t in range(TT):
                        maximum(0, 0, t)
                produce(pro, name)
            pe.wait_ge(job_hi, pro.done(HI, ("k", 0)))
            for t in range(TT // 2):
                maximum(0, 1, t)
            pe.wait_ge(const_dve, 3)
            row(0, 0)

            def slot(it, h, t):
                b, kind = it.b, it.kind
                p, ahead = h // 2, (h + 2) // 2 % PAIRS
                if h % 2 == 0 and t == 0:
                    pe.wait_ge(job_free, (it.done if p else it.done_before)(JOBS, ("k", p)) + BANKS)
                    pe.wait_ge(q_dup[p % 2], dup_count(b, p))
                    pe.wait_ge(k_dup[p % 2], dup_count(b, p))
                if t == 0:
                    pe.wait_ge(st_free, row_count(b, h) + 2)
                for part in PE_ORDER[h % 2][t].split():
                    if part == "scores":
                        scores(b, h, t)
                    elif part == "maximum":
                        if maximum_at(kind, h, t):
                            if h % 2 == 0 and t == TT // 2:
                                pe.wait_ge(job_hi, it.done(HI, ("k", ahead)))
                            maximum(b, *maximum_at(kind, h, t))
                    elif part == "values":
                        if t == VALUES_SLOT and (h >= VALUES_BACK or kind != FIRST):
                            values(b, h - VALUES_BACK)
                    elif part == "jobs":
                        for name in jobs_of(kind, h, t):
                            produce(it, name)
                    elif part == "row":
                        if t == ROW_UNIT - 1 and (h + 1 < HEADS or kind != LAST):
                            row(b, h + 1)

            run(pe, slot=slot)
            epi = Iteration(EPI, BATCHES)
            values(BATCHES - 1, HEADS - 2)
            values(BATCHES - 1, HEADS - 1)
            for name in JOBS[EPI]:
                produce(epi, name)


def kernel(x, ctx_512, g_xattn, g_ffn, L0_xattn_Wq, L0_xattn_Wk, L0_xattn_Wv, L0_xattn_Wo, L0_xattn_bo,
           L0_ffn_gate_w, L0_ffn_expert_w, L0_ffn_expert_b):
    import numpy as np
    import concourse.bacc as bacc
    from concourse.bass_utils import run_bass_kernel_spmd

    nc = bacc.Bacc("TRN2", target_bir_lowering=False, num_devices=1)
    ins = {
        "x": x,
        "kv_t": np.asarray(ctx_512).transpose(0, 2, 1),
        "g_xattn": g_xattn,
        "g_ffn": g_ffn,
        "wq": L0_xattn_Wq, "wk": L0_xattn_Wk, "wv": L0_xattn_Wv, "wo": L0_xattn_Wo, "bo": L0_xattn_bo,
        "gate_t": np.asarray(L0_ffn_gate_w).T,
        "expert_t": np.asarray(L0_ffn_expert_w).transpose(2, 0, 1).reshape(DIM, EXPERTS * DIM),
        "expert_b": L0_ffn_expert_b,
    }
    ins = {n: np.ascontiguousarray(a) for n, a in ins.items()}
    aps = {n: nc.dram_tensor(n, a.shape, mybir.dt.from_np(a.dtype), kind="ExternalInput").ap()
           for n, a in ins.items()}
    out = nc.dram_tensor("out", (BATCHES, TOKENS, DIM), F32, kind="ExternalOutput").ap()
    build(nc, out=out, **aps)
    r = run_bass_kernel_spmd(nc, [ins], core_ids=[0])
    return r.results[0]["out"]
```
